# Optimizing a Trainium2 kernel written in Bass

```python
import numpy as np
import jax
import jax.numpy as jnp

def _softmax(x, axis=-1):
    return jax.nn.softmax(x, axis=axis)

def _gelu(x):
    return jax.nn.gelu(x, approximate=True)

def _silu(x):
    return jax.nn.silu(x)

def _sigmoid(x):
    return jax.nn.sigmoid(x)

def _layernorm(x, axis=-1, eps=1e-05):
    m = jnp.mean(x, axis=axis, keepdims=True)
    v = jnp.var(x, axis=axis, keepdims=True)
    return (x - m) / jnp.sqrt(v + eps)

def _scatter_add(tgt, idx, src, axis=0):
    return tgt.at[idx].add(src)

def _segment_sum(src, seg, n):
    return jax.ops.segment_sum(src, seg, n)
kernel_name = 'mk_conv_attn_hybrid_d2_conv_nchw512_r4_58bc52'

def setup_inputs(seed: int=0):
    np.random.seed(seed)
    _w = jnp.asarray

    def _rec_inputs():
        import jax
        import jax.numpy as jnp
        _gk = jax.random.key(seed)
        x = -0.000125 + 0.9999 * jax.random.normal(jax.random.fold_in(_gk, 1), (16, 128, 32, 32), jnp.float32)
        return x
    x = _rec_inputs()

    def _L0_conv_setup():
        import jax, jax.numpy as jnp
        import numpy as np
        NS = 8
        MAPPER_X = [0, 0, 1, -1, 0, 3, 0, 2]
        MAPPER_Y = [0, 1, 0, -1, 3, 0, 2, 0]

        def build_dct_weight(C, H, W):

            def basis(L, freq):
                pos = np.arange(L)
                r = np.cos(np.pi * freq * (pos + 0.5) / L) / np.sqrt(L)
                return r * np.sqrt(2.0) if freq != 0 else r
            c_part = C // NS
            w = np.zeros((C, H, W), np.float32)
            for i, (u, v) in enumerate(zip(MAPPER_X, MAPPER_Y)):
                w[i * c_part:(i + 1) * c_part] = np.outer(basis(H, u), basis(W, v)).astype(np.float32)
            return jnp.asarray(w)
        key = jax.random.key(seed)
        k1, k2, k3, k4, k5 = jax.random.split(key, 5)
        N, C, H, W = (16, 128, 32, 32)
        c_part = C // NS
        hid = C // 16
        return {'x': jax.random.normal(k1, (N, C, H, W), jnp.float32), 'W1': jax.random.normal(k2, (NS, hid, c_part), jnp.float32) * 0.05, 'W2': jax.random.normal(k3, (NS, c_part, hid), jnp.float32) * 0.05, 'M1': jax.random.normal(k4, (NS, NS), jnp.float32) * 0.3, 'M2': jax.random.normal(k5, (NS, NS), jnp.float32) * 0.3}
    _L0_conv_all = _L0_conv_setup()
    _L0_conv_in = {k: v for k, v in _L0_conv_all.items() if k in ('W1', 'W2', 'M1', 'M2')}
    del _L0_conv_all

    def _L1_attn_setup():
        import jax, jax.numpy as jnp
        import numpy as np
        import math
        HEADS = 8
        DIM_HEAD = 16
        key = jax.random.key(seed)
        k1, k2, k3 = jax.random.split(key, 3)
        b, n, dim = (4, 512, 128)
        inner = HEADS * DIM_HEAD
        x = jax.random.normal(k1, (b, n, dim), dtype=jnp.float32)
        W_qkv = jax.random.normal(k2, (dim, 4 * inner), dtype=jnp.float32) * dim ** (-0.5)
        W_out = jax.random.normal(k3, (2 * inner, dim), dtype=jnp.float32) * (2 * inner) ** (-0.5)
        b_out = jnp.zeros((dim,), dtype=jnp.float32)
        return {'x': x, 'W_qkv': W_qkv, 'W_out': W_out, 'b_out': b_out}
    _L1_attn_all = _L1_attn_setup()
    _L1_attn_in = {k: v for k, v in _L1_attn_all.items() if k in ('W_qkv', 'W_out', 'b_out')}
    del _L1_attn_all

    def _L1_ffn_setup():
        import jax, jax.numpy as jnp
        import numpy as np
        NUM_EXPERTS = 8
        TOP_K = 2
        key = jax.random.key(seed)
        ks = jax.random.split(key, 4)
        B, S, D, F, E = (4, 1024, 128, 256, NUM_EXPERTS)
        x = jax.random.normal(ks[0], (B, S, D), dtype=jnp.float32)
        w1 = jax.random.normal(ks[1], (E, D, F), dtype=jnp.float32) * 0.02
        b1 = jnp.zeros((E, F), dtype=jnp.float32)
        w2 = jax.random.normal(ks[2], (E, F, D), dtype=jnp.float32) * 0.02
        b2 = jnp.zeros((E, D), dtype=jnp.float32)
        wg = jax.random.normal(ks[3], (D, E), dtype=jnp.float32) * 0.02
        bg = jnp.zeros((E,), dtype=jnp.float32)
        return {'x': x, 'w1': w1, 'b1': b1, 'w2': w2, 'b2': b2, 'wg': wg, 'bg': bg}
    _L1_ffn_all = _L1_ffn_setup()
    _L1_ffn_in = {k: v for k, v in _L1_ffn_all.items() if k in ('w1', 'b1', 'w2', 'b2', 'wg', 'bg')}
    del _L1_ffn_all
    return {'x': x, 'L0_conv_W1': _L0_conv_in['W1'], 'L0_conv_W2': _L0_conv_in['W2'], 'L0_conv_M1': _L0_conv_in['M1'], 'L0_conv_M2': _L0_conv_in['M2'], 'L1_attn_W_qkv': _L1_attn_in['W_qkv'], 'L1_attn_W_out': _L1_attn_in['W_out'], 'L1_attn_b_out': _L1_attn_in['b_out'], 'L1_ffn_w1': _L1_ffn_in['w1'], 'L1_ffn_b1': _L1_ffn_in['b1'], 'L1_ffn_w2': _L1_ffn_in['w2'], 'L1_ffn_b2': _L1_ffn_in['b2'], 'L1_ffn_wg': _L1_ffn_in['wg'], 'L1_ffn_bg': _L1_ffn_in['bg']}

def reference(x, L0_conv_W1, L0_conv_W2, L0_conv_M1, L0_conv_M2, L1_attn_W_qkv, L1_attn_W_out, L1_attn_b_out, L1_ffn_w1, L1_ffn_b1, L1_ffn_w2, L1_ffn_b2, L1_ffn_wg, L1_ffn_bg):
    import jax
    import jax.numpy as jnp

    def _L0_conv_ref(x, W1, W2, M1, M2):
        import jax, jax.numpy as jnp
        import numpy as np
        NS = 8
        MAPPER_X = [0, 0, 1, -1, 0, 3, 0, 2]
        MAPPER_Y = [0, 1, 0, -1, 3, 0, 2, 0]

        def build_dct_weight(C, H, W):

            def basis(L, freq):
                pos = np.arange(L)
                r = np.cos(np.pi * freq * (pos + 0.5) / L) / np.sqrt(L)
                return r * np.sqrt(2.0) if freq != 0 else r
            c_part = C // NS
            w = np.zeros((C, H, W), np.float32)
            for i, (u, v) in enumerate(zip(MAPPER_X, MAPPER_Y)):
                w[i * c_part:(i + 1) * c_part] = np.outer(basis(H, u), basis(W, v)).astype(np.float32)
            return jnp.asarray(w)
        n, c, h, w = x.shape
        c_part = c // NS
        dct_w = build_dct_weight(c, h, w)
        dct_freq = jnp.einsum('nchw,chw->nc', x, dct_w)
        m = dct_freq.reshape(n, NS, c_part).mean(axis=2)
        freq_weight = jax.nn.sigmoid(jax.nn.relu(m @ M1.T) @ M2.T)
        g = dct_freq.reshape(n, NS, c_part)
        hgate = jax.nn.relu(jnp.einsum('ngc,goc->ngo', g, W1))
        att = jax.nn.sigmoid(jnp.einsum('ngo,gco->ngc', hgate, W2))
        scale = (att * freq_weight[:, :, None]).reshape(n, c)
        return scale[:, :, None, None] * x

    def _L1_attn_ref(x, W_qkv, W_out, b_out):
        import jax, jax.numpy as jnp
        import numpy as np
        import math
        HEADS = 8
        DIM_HEAD = 16
        b, n, d = x.shape
        h, dh = (HEADS, DIM_HEAD)
        scale = dh ** (-0.5)
        qkvt = x @ W_qkv
        q, k, v, t = jnp.split(qkvt, 4, axis=-1)

        def to_heads(z):
            return z.reshape(b, n, h, dh).transpose(0, 2, 1, 3)
        q, k, v, t = map(to_heads, (q, k, v, t))
        dots = jnp.einsum('bhid,bhjd->bhij', q, k) * scale
        attn1 = jax.nn.softmax(dots, axis=-1)
        out1 = jnp.einsum('bhij,bhjd->bhid', attn1, v)
        pos = jnp.arange(1, n + 1, dtype=x.dtype)
        tg = jnp.abs(pos[None, :] - pos[:, None])
        attn2 = jnp.exp(-tg / jnp.asarray(math.e, dtype=x.dtype))
        attn2 = attn2 / attn2.sum(-1)
        out2 = jnp.einsum('ij,bhjd->bhid', attn2, t)
        out = jnp.concatenate([out1, out2], axis=-1)
        out = out.transpose(0, 2, 1, 3).reshape(b, n, 2 * h * dh)
        return out @ W_out + b_out

    def _L1_ffn_ref(x, w1, b1, w2, b2, wg, bg):
        import jax, jax.numpy as jnp
        import numpy as np
        NUM_EXPERTS = 8
        TOP_K = 2
        B, S, D = x.shape
        E = wg.shape[1]
        xf = x.reshape(-1, D)
        logits = xf @ wg + bg
        top_vals, top_idx = jax.lax.top_k(logits, TOP_K)
        gate_w = jax.nn.softmax(top_vals, axis=-1)
        onehot = jax.nn.one_hot(top_idx, E, dtype=x.dtype)
        combine = jnp.einsum('tke,tk->te', onehot, gate_w)
        h = jax.nn.relu(jnp.einsum('td,edf->etf', xf, w1) + b1[:, None, :])
        y = jnp.einsum('etf,efd->etd', h, w2) + b2[:, None, :]
        out = jnp.einsum('etd,te->td', y, combine)
        return out.reshape(B, S, D)

    def _gn(v, G=32, eps=1e-05):
        B_, C_, H_, W_ = v.shape
        g = v.reshape(B_, G, C_ // G, H_, W_)
        m = jnp.mean(g, axis=(2, 3, 4), keepdims=True)
        s = jnp.var(g, axis=(2, 3, 4), keepdims=True)
        return ((g - m) / jnp.sqrt(s + eps)).reshape(v.shape)

    def _ln_c(v, eps=1e-06):
        m = jnp.mean(v, axis=1, keepdims=True)
        s = jnp.var(v, axis=1, keepdims=True)
        return (v - m) / jnp.sqrt(s + eps)

    def _ln_t(v, eps=1e-05):
        m = jnp.mean(v, axis=-1, keepdims=True)
        s = jnp.var(v, axis=-1, keepdims=True)
        return (v - m) / jnp.sqrt(s + eps)

    def _to_tokens(v):
        B_, C_, H_, W_ = v.shape
        return v.reshape(B_, C_, H_ * W_).transpose(0, 2, 1)

    def _from_tokens(t, like):
        B_, C_, H_, W_ = like.shape
        return t.transpose(0, 2, 1).reshape(B_, C_, H_, W_)
    x = x + _L0_conv_ref(_gn(x), L0_conv_W1, L0_conv_W2, L0_conv_M1, L0_conv_M2)
    t = _to_tokens(x)
    t = t + _L1_attn_ref(_ln_t(t), L1_attn_W_qkv, L1_attn_W_out, L1_attn_b_out)
    t = t + _L1_ffn_ref(_ln_t(t), L1_ffn_w1, L1_ffn_b1, L1_ffn_w2, L1_ffn_b2, L1_ffn_wg, L1_ffn_bg)
    x = _from_tokens(t, x)
    return x

_drawn_inputs = setup_inputs


def setup_inputs(seed=0):
    import zlib

    import numpy as np

    out = dict(_drawn_inputs(seed))
    spreads = {'L1_attn_b_out': (0.0, 0.1),
     'L1_ffn_b1': (0.0, 0.642),
     'L1_ffn_b2': (0.0, 0.1),
     'L1_ffn_bg': (0.0, 0.1)}
    factors = {'L0_conv_W1': 8.0, 'L0_conv_W2': 8.0, 'L0_conv_M1': 6.409, 'L0_conv_M2': 5.208}
    for name, (base, spread) in spreads.items():
        noise = np.random.default_rng([zlib.crc32(name.encode()), seed]).standard_normal(out[name].shape)
        drawn = base * np.exp(spread * noise) if base else spread * noise
        out[name] = jnp.asarray(drawn.astype(out[name].dtype))
    for name, factor in factors.items():
        out[name] = (out[name] * factor).astype(out[name].dtype)
    return out
```

```python
from contextlib import ExitStack

import numpy as np

import concourse.bass as bass
from concourse import mybir

F32 = mybir.dt.float32
BF16 = mybir.dt.bfloat16
ALU = mybir.AluOpType
ACT = mybir.ActivationFunctionType
AX = mybir.AxisListType

P = 128
IMAGES = 16
SIDE = 32
TOK = SIDE * SIDE
TILES = TOK // P
BANK = 512
HALVES = TOK // BANK
HEADS, DH = 8, 16
GROUP = 4
GROUPS = HEADS // GROUP
SPLITS = 8
CP_SPLIT = P // SPLITS
HID = P // 16
NORM_GROUP = 4
EXPERTS, FF = 8, 256
FT = FF // P
SLICES = EXPERTS * FT
REACH = 2
STRIP = (2 * REACH + 1) * P
Q_PARTS = (0, 0, 1, 0, 2, 1)
K_PARTS = (0, 1, 0, 2, 0, 1)
PAIRS = len(Q_PARTS)
SHIFT_ROW = PAIRS * DH
STACK = SHIFT_ROW + 3
DCT_X = (0, 0, 1, -1, 0, 3, 0, 2)
DCT_Y = (0, 1, 0, -1, 3, 0, 2, 0)


def shape_constants():
    def basis(freq):
        r = np.cos(np.pi * freq * (np.arange(SIDE) + 0.5) / SIDE) / np.sqrt(SIDE)
        return r * np.sqrt(2.0) if freq != 0 else r

    c = {}
    dct = np.zeros((P, SIDE, SIDE), np.float32)
    for i, (u, v) in enumerate(zip(DCT_X, DCT_Y)):
        dct[i * CP_SPLIT:(i + 1) * CP_SPLIT] = np.outer(basis(u), basis(v)).astype(np.float32)
    c["dct"] = dct.reshape(P, TOK)
    c["dct_sum"] = dct.astype(np.float64).sum((1, 2)).astype(np.float32).reshape(P, 1)
    ch = np.arange(P)
    c["ident"] = np.eye(P, dtype=np.float32)
    c["group_mean"] = (ch[:, None] // NORM_GROUP == ch[None] // NORM_GROUP).astype(np.float32) / NORM_GROUP
    member = (ch[:, None] // CP_SPLIT == np.arange(SPLITS)[None]).astype(np.float32)
    c["split_mean"] = member / CP_SPLIT
    c["split_spread"] = np.ascontiguousarray(member.T)
    c["sum_spread"] = ((ch[:, None] % 32 == DH) & (ch[:, None] // 32 == ch[None] // 32)).astype(np.float32)
    dist = np.abs(np.arange(STRIP)[None] - REACH * P - ch[:, None]).astype(np.float32)
    c["decay"] = np.exp(-dist / np.float32(np.e)).astype(np.float32)
    pos = np.arange(TOK, dtype=np.float32)
    full = np.exp(-np.abs(pos[None] - pos[:, None]) / np.float32(np.e)).astype(np.float32)
    c["decay_norm"] = np.ascontiguousarray((1.0 / full.sum(-1)).astype(np.float32).reshape(TILES, P).T)
    pick = np.zeros((3, EXPERTS, EXPERTS, P), np.float32)
    for e in range(EXPERTS):
        pick[:, e, e] = 1.0
    c["gate_pick"] = pick.reshape(3 * EXPERTS, EXPERTS * P)
    c["rank"] = np.tile((EXPERTS - np.arange(EXPERTS)).astype(np.float32), (P, TILES))
    return {k: np.ascontiguousarray(v, dtype=np.float32) for k, v in c.items()}


def build(nc, a, out):
    nc.disable_value_cache = True
    with ExitStack() as ctx:
        def sb(name, shape, dt=F32):
            return ctx.enter_context(nc.sbuf_tensor(name, shape, dt))

        def sem(name):
            return ctx.enter_context(nc.semaphore(name))

        dct = sb("dct", [P, TOK])
        dct_sum = sb("dct_sum", [P, 1])
        ident = sb("ident", [P, P])
        group_mean = sb("group_mean", [P, P])
        split_mean = sb("split_mean", [P, SPLITS])
        split_spread = sb("split_spread", [SPLITS, P])
        sum_spread = sb("sum_spread", [P, P])
        decay = sb("decay", [P, STRIP])
        decay_norm = sb("decay_norm", [P, TILES])
        rank = sb("rank", [P, TILES * EXPERTS])
        pick_bf = sb("pick_bf", [3 * EXPERTS, EXPERTS * P], BF16)
        m1_t = sb("m1_t", [SPLITS, SPLITS])
        m2_t = sb("m2_t", [SPLITS, SPLITS])
        w1_blocks = sb("w1_blocks", [P, SPLITS * HID])
        w2_blocks = sb("w2_blocks", [SPLITS * HID, P])
        wq = sb("wq", [P, P])
        wk = sb("wk", [P, P])
        wvz = sb("wvz", [P, 2 * P])
        wt_t = sb("wt_t", [P, P])
        wo2 = sb("wo2", [P, P])
        wo1 = sb("wo1", [P, GROUPS, P])
        b_out = sb("b_out", [P, 1])
        w_in = sb("w_in", [P, SLICES, P])
        w_out = sb("w_out", [P, SLICES, P])
        b1 = sb("b1", [P, SLICES])
        neg_b1 = sb("neg_b1", [P, SLICES])
        b2_t = sb("b2_t", [P, EXPERTS])
        w_gate = sb("w_gate", [P, EXPERTS])
        b_gate = sb("b_gate", [P, TILES * EXPERTS])
        bias3 = sb("bias3", [P, 3, EXPERTS])
        bias_rows = sb("bias_rows", [3 * EXPERTS, P])
        minus_half = sb("minus_half", [P, IMAGES])

        stat13 = sb("stat13", [P, 2, 13])
        moments = sb("moments", [P, IMAGES, 2])
        ttr_out = sb("ttr_out", [P, TOK])
        stats = sb("stats", [P, IMAGES, 13])
        se = sb("se", [P, 12, IMAGES])
        slope = sb("slope", [P, IMAGES])
        offset = sb("offset", [P, IMAGES])

        x_in = sb("x_in", [P, 2, TOK])
        x1 = sb("x1", [P, TOK])
        norm6 = sb("norm6", [P, TILES, 6])
        norm_v = sb("norm_v", [P, 7, TILES])
        norm_rs = sb("norm_rs", [P, TILES])
        norm_tok = sb("norm_tok", [P, TILES, P])
        norm_ch = sb("norm_ch", [P, TOK])
        q_parts = sb("q_parts", [P, 3, TOK], BF16)
        k_parts = sb("k_parts", [P, 3, TOK], BF16)
        rest = sb("rest", [P, TOK])
        q_stack = sb("q_stack", [STACK, HEADS, TOK], BF16)
        k_stack = sb("k_stack", [STACK, HEADS, TOK], BF16)
        v_aug = sb("v_aug", [P, TILES, HEADS, 32])
        z = sb("z", [P, TILES, P])
        row_max = sb("row_max", [P, HEADS * TILES])
        max_parts = sb("max_parts", [HEADS * TILES, 3, P], BF16)
        max_rest = sb("max_rest", [HEADS * TILES, P])
        probs = sb("probs", [P, 2, GROUP, TOK])
        o_sb = sb("o_sb", [P, GROUPS, TOK])
        t2 = sb("t2", [P, TOK])
        gate = sb("gate", [P, 8, TILES * EXPERTS])
        gate_v = sb("gate_v", [P, 8, TILES])
        gate_bf = sb("gate_bf", [P, TILES * EXPERTS], BF16)
        gate3 = sb("gate3", [P, TILES, 3, EXPERTS])
        gate_t = sb("gate_t", [3 * EXPERTS, TOK])
        gate_t_bf = sb("gate_t_bf", [3 * EXPERTS, TOK], BF16)
        gate_wide = sb("gate_wide", [P, 3, BANK])
        hidden = sb("hidden", [P, 4, BANK])
        result = sb("result", [P, TOK])

        ps = ctx.enter_context(nc.psum_tensor("ps", [P, 8, BANK], F32))

        const_in = sem("const_in")
        x_setup_in = sem("x_setup_in")
        stats_done = sem("stats_done")
        setup_pe = sem("setup_pe")
        setup_dve = sem("setup_dve")
        setup_act = sem("setup_act")
        setup_pool = sem("setup_pool")
        setup_chain = sem("setup_chain")
        setup_done = sem("setup_done")
        bn_done = sem("bn_done")
        dot_done = sem("dot_done")
        aggr_done = sem("aggr_done")
        picks_in = sem("picks_in")
        x_loaded = sem("x_loaded")
        x1_done = sem("x1_done")
        turned = sem("turned")
        dve_bn = sem("dve_bn")
        dve_norm = sem("dve_norm")
        rs_done = sem("rs_done")
        tok_done = sem("tok_done")
        back = sem("back")
        norm_done = sem("norm_done")
        qk_ready = sem("qk_ready")
        qk_high = sem("qk_high")
        qk_split = sem("qk_split")
        dve_split = sem("dve_split")
        vz_ready = sem("vz_ready")
        vz_done = sem("vz_done")
        stack_in = sem("stack_in")
        full_ready = sem("full_ready")
        max_done = sem("max_done")
        max_turned = sem("max_turned")
        dve_max = sem("dve_max")
        dve_mid = sem("dve_mid")
        max_split = sem("max_split")
        shift_in = sem("shift_in")
        score_ready = sem("score_ready")
        exp_done = sem("exp_done")
        value_done = sem("value_done")
        o_copied = sem("o_copied")
        sums_wide = sem("sums_wide")
        dve_o = sem("dve_o")
        o_scaled = sem("o_scaled")
        attn_ready = sem("attn_ready")
        t2_done = sem("t2_done")
        logits_ready = sem("logits_ready")
        dve_gate = sem("dve_gate")
        gap_done = sem("gap_done")
        gap_exp = sem("gap_exp")
        gates_done = sem("gates_done")
        gates_turned = sem("gates_turned")
        gates_copied = sem("gates_copied")
        wide_ready = sem("wide_ready")
        wide_done = sem("wide_done")
        hidden_ready = sem("hidden_ready")
        hidden_done = sem("hidden_done")
        hidden_used = sem("hidden_used")
        result_done = sem("result_done")
        stored = sem("stored")

        STEPS = HEADS * TILES
        QUADS = GROUPS * TILES
        FFN_STEPS = HALVES * SLICES
        WIDES = HALVES * EXPERTS
        STACK_INC = 2 * PAIRS * HEADS * 16
        SHIFT_INC = 3 * 16
        STORE_INC = HALVES * 16
        NORM_CHAIN, SPLIT_CHAIN, MAX_CHAIN, O_CHAIN, GATE_CHAIN = 4, 2, 2, 1, 24

        consts = [(dct, "dct"), (dct_sum, "dct_sum"), (ident, "ident"), (group_mean, "group_mean"),
                  (split_mean, "split_mean"), (split_spread, "split_spread"), (sum_spread, "sum_spread"),
                  (decay, "decay"), (decay_norm, "decay_norm"), (rank, "rank"), (m1_t, "m1_t"), (m2_t, "m2_t"),
                  (w1_blocks, "w1_blocks"), (w2_blocks, "w2_blocks"), (wq, "wq"), (wk, "wk"),
                  (wt_t, "wt_t"), (wo2, "wo2"), (b_out, "b_out"), (b1, "b1"), (b2_t, "b2_t"),
                  (w_gate, "w_gate")]
        CONST_INC = 16 * (len(consts) + 6)

        def banks(lo, n):
            return ps[:, lo:lo + n, :]

        def flat(lo):
            return ps[:, lo:lo + 2, :].rearrange("p a b -> p (a b)")

        def tiles(lo):
            return ps[:, lo:lo + 2, :].rearrange("p a (b c) -> p (a b) c", c=P)

        block = ctx.enter_context(nc.Block())

        @block.sync
        def _(sp):
            for tile, name in consts:
                sp.dma_start(tile[:, :], a[name]).then_inc(const_in, 16)
            sp.dma_start(wvz[:, 0:P], a["wv"]).then_inc(const_in, 16)
            sp.dma_start(wo1[:, :, :], a["wo1"]).then_inc(const_in, 16)
            sp.dma_start(w_in[:, :, :], a["w_in"]).then_inc(const_in, 16)
            sp.dma_start(w_out[:, :, :], a["w_out"]).then_inc(const_in, 16)
            sp.dma_start(b_gate[:, :].rearrange("p (t e) -> p t e", t=TILES),
                         a["b_gate"].unsqueeze(0).broadcast_to([P, TILES, EXPERTS])).then_inc(const_in, 16)
            sp.dma_start(ttr_out[0:3 * EXPERTS, :], a["gate_pick"]).then_inc(const_in, 16)
            with sp.Fori(0, IMAGES) as b:
                before = sp.snap(b * STEPS)
                for n, (stack, parts, order) in enumerate(((q_stack, q_parts, Q_PARTS), (k_stack, k_parts, K_PARTS))):
                    sp.wait_ge(score_ready, before)
                    sp.wait_ge(qk_split, b * 2 + n + 1)
                    for j, part in enumerate(order):
                        for h in range(HEADS):
                            sp.dma_start(stack[j * DH:(j + 1) * DH, h, :],
                                         parts[h * DH:(h + 1) * DH, part, :]).then_inc(stack_in, 16)
                sp.wait_ge(max_split, b + 1)
                for j in range(3):
                    sp.dma_start(q_stack[SHIFT_ROW + j:SHIFT_ROW + j + 1, :, :]
                                 .rearrange("p h (t q) -> p (h t) q", q=P),
                                 max_parts[:, j, :]).then_inc(shift_in, 16)

        @block.gpsimd
        def _(pool):
            pool.memset(minus_half[:, :], -0.5).then_inc(setup_pool, 1)
            pool.memset(v_aug[:, :, :, :], 0.0).then_inc(setup_pool, 1)
            pool.wait_ge(setup_pool, 2)
            pool.memset(v_aug[:, :, :, DH:DH + 1], 1.0).then_inc(setup_pool, 1)
            pool.wait_ge(setup_pool, 3)
            pool.wait_ge(setup_dve, 3)
            pool.tensor_tensor(se[:, 4, :], se[:, 3, :], minus_half[:, :], ALU.pow).then_inc(setup_pool, 1)
            with pool.Fori(0, IMAGES) as b:
                for k in range(2):
                    pool.wait_ge(dve_norm, (b * 2 + k + 1) * NORM_CHAIN)
                    pool.tensor_tensor(norm_rs[:, :], norm_v[:, 6, :], minus_half[:, 0:TILES],
                                       ALU.pow).then_inc(rs_done, 1)

        @block.tensor
        def _(pe):
            def small(bank, rows, cols, lhs_t, rhs):
                return pe.matmul(ps[0:rows, bank, 0:cols], lhs_t, rhs, start=True, stop=True)

            pe.wait_ge(const_in, CONST_INC)
            pe.wait_ge(setup_dve, 1)
            small(0, P, IMAGES, group_mean[:, :], se[:, 0, :]).then_inc(setup_pe, 1)
            pe.wait_ge(setup_dve, 2)
            small(1, P, IMAGES, group_mean[:, :], se[:, 2, :]).then_inc(setup_pe, 1)
            pe.wait_ge(setup_dve, 4)
            small(2, SPLITS, IMAGES, split_mean[:, :], se[:, 5, :]).then_inc(setup_pe, 1)
            pe.wait_ge(setup_dve, 5)
            small(3, SPLITS, IMAGES, m1_t[:, :], se[0:SPLITS, 6, :]).then_inc(setup_pe, 1)
            small(4, SPLITS * HID, IMAGES, w1_blocks[:, :], se[:, 5, :]).then_inc(setup_pe, 1)
            pe.wait_ge(setup_dve, 6)
            small(5, SPLITS, IMAGES, m2_t[:, :], se[0:SPLITS, 7, :]).then_inc(setup_pe, 1)
            pe.wait_ge(setup_dve, 7)
            small(6, P, IMAGES, w2_blocks[:, :], se[0:SPLITS * HID, 8, :]).then_inc(setup_pe, 1)
            pe.wait_ge(setup_dve, 8)
            small(7, P, IMAGES, split_spread[:, :], se[0:SPLITS, 9, :]).then_inc(setup_pe, 1)
            small(0, P, P, wt_t[:, :], wo2[:, :]).then_inc(setup_pe, 1)
            for e in range(EXPERTS):
                for f in range(FT):
                    n = e * FT + f
                    mm = pe.matmul(ps[:, 1, e:e + 1], w_out[:, n, :], b1[:, n:n + 1], start=(f == 0), stop=(f == FT - 1))
            mm.then_inc(setup_pe, 1)
            pe.wait_ge(setup_dve, 10)
            small(2, 3 * EXPERTS, P, bias3[:, :, :].rearrange("p a b -> p (a b)"), ident[:, :]).then_inc(setup_pe, 1)

            def turn(b, k, src):
                for t in range(TILES):
                    mm = pe.transpose(tiles(0)[:, t, :], src[:, t * P:(t + 1) * P], ident[:, :])
                mm.then_inc(turned, 1)
                pe.wait_ge(tok_done, b * 2 + k + 1)
                for t in range(TILES):
                    mm = pe.transpose(tiles(2)[:, t, :], norm_tok[:, t, :], ident[:, :])
                mm.then_inc(back, 1)
                pe.wait_ge(norm_done, b * 2 + k + 1)

            pe.wait_ge(setup_done, 1)
            pe.wait_ge(setup_pool, 3)
            with pe.Fori(0, IMAGES) as b:
                pe.wait_ge(x1_done, b + 1)
                pe.wait_ge(hidden_done, b * FFN_STEPS)
                turn(b, 0, x1)
                pe.wait_ge(wide_done, b * WIDES)
                pe.wait_ge(result_done, b * HALVES)
                for n, w in enumerate((wq, wk)):
                    for c in range(HALVES):
                        mm = pe.matmul(ps[:, 4 + 2 * n + c, :], w[:, :], norm_ch[:, c * BANK:(c + 1) * BANK],
                                       start=True, stop=True)
                    mm.then_inc(qk_ready, 1)
                for t in range(TILES):
                    mm = pe.matmul(ps[:, t // 2, (t % 2) * 2 * P:(t % 2 + 1) * 2 * P], norm_ch[:, t * P:(t + 1) * P],
                                   wvz[:, :], start=True, stop=True)
                    if t % 2:
                        mm.then_inc(vz_ready, 1)
                pe.wait_ge(stack_in, (b + 1) * STACK_INC)
                pe.wait_ge(vz_done, (b + 1) * 4)
                pe.wait_ge(qk_split, (b + 1) * 2)
                for n in range(STEPS):
                    h, t = divmod(n, TILES)
                    if n >= 4:
                        pe.wait_ge(max_done, b * STEPS + n - 3)
                    for c in range(HALVES):
                        mm = pe.matmul(ps[:, 2 * (n % 4) + c, :], q_stack[0:SHIFT_ROW, h, t * P:(t + 1) * P],
                                       k_stack[0:SHIFT_ROW, h, c * BANK:(c + 1) * BANK], start=True, stop=True)
                    mm.then_inc(full_ready, 1)
                pe.wait_ge(max_done, (b + 1) * STEPS)
                pe.matmul(ps[0:STEPS, 0, 0:P], row_max[:, :], ident[:, :], start=True, stop=True).then_inc(max_turned, 1)
                pe.wait_ge(shift_in, (b + 1) * SHIFT_INC)

                def scores(s):
                    g, r = divmod(s, TILES * GROUP)
                    t, i = divmod(r, GROUP)
                    h = g * GROUP + i
                    if s >= 3:
                        pe.wait_ge(exp_done, b * STEPS + s - 2)
                    for c in range(HALVES):
                        mm = pe.matmul(ps[:, 2 * (s % 3) + c, :], k_stack[:, h, t * P:(t + 1) * P],
                                       q_stack[:, h, c * BANK:(c + 1) * BANK], start=True, stop=True)
                    mm.then_inc(score_ready, 1)

                def values(u, c):
                    g, t = divmod(u, TILES)
                    if c == 0:
                        pe.wait_ge(exp_done, b * STEPS + (u + 1) * GROUP)
                        if u == TILES:
                            pe.wait_ge(o_copied, b * GROUPS + 1)
                    for i in range(GROUP):
                        mm = pe.matmul(ps[32 * i:32 * i + 32, 6 + c, :], v_aug[:, t, g * GROUP + i, :],
                                       probs[:, u % 2, i, c * BANK:(c + 1) * BANK],
                                       start=(t == 0), stop=(t == TILES - 1))
                    if c == HALVES - 1:
                        mm.then_inc(value_done, 1)

                for s in range(GROUP + 2):
                    scores(s)
                for u in range(QUADS):
                    s = (u + 1) * GROUP + 2
                    values(u, 0)
                    if s < STEPS:
                        scores(s)
                    values(u, 1)
                    for k in range(s + 1, min(s + GROUP, STEPS)):
                        scores(k)
                pe.wait_ge(o_copied, b * GROUPS + 2)
                for t in range(TILES):
                    near = range(max(0, t - REACH), min(TILES, t + REACH + 1))
                    for kt in near:
                        at = (t - kt + REACH) * P
                        pe.matmul(ps[:, 6 + t // 4, (t % 4) * P:(t % 4 + 1) * P], z[:, kt, :], decay[:, at:at + P],
                                  start=(t % 4 == 0 and kt == near[0]), stop=False)
                pe.wait_ge(exp_done, (b + 1) * STEPS)
                for g in range(GROUPS):
                    for c in range(HALVES):
                        mm = pe.matmul(ps[:, 2 * g + c, :], sum_spread[:, :], o_sb[:, g, c * BANK:(c + 1) * BANK],
                                       start=True, stop=True)
                    mm.then_inc(sums_wide, 1)
                for g in range(GROUPS):
                    pe.wait_ge(o_scaled, b * GROUPS + g + 1)
                    for c in range(HALVES):
                        mm = pe.matmul(ps[:, 6 + c, :], wo1[:, g, :], o_sb[:, g, c * BANK:(c + 1) * BANK],
                                       start=False, stop=(g == GROUPS - 1))
                mm.then_inc(attn_ready, 1)
                pe.wait_ge(t2_done, b + 1)
                turn(b, 1, t2)
                for t in range(TILES):
                    mm = pe.matmul(ps[:, 4, t * EXPERTS:(t + 1) * EXPERTS], norm_ch[:, t * P:(t + 1) * P], w_gate[:, :],
                                   start=True, stop=True)
                mm.then_inc(logits_ready, 1)

                def first(m):
                    c, n = divmod(m, SLICES)
                    if m >= 4:
                        pe.wait_ge(hidden_done, b * FFN_STEPS + m - 3)
                    pe.matmul(ps[:, m % 4, :], w_in[:, n, :], norm_ch[:, c * BANK:(c + 1) * BANK],
                              start=True, stop=True).then_inc(hidden_ready, 1)

                def wide(w):
                    c, e = divmod(w, EXPERTS)
                    if w >= 2:
                        pe.wait_ge(wide_done, b * WIDES + w - 1)
                    pe.matmul(ps[:, 4 + w % 2, :], pick_bf[:, e * P:(e + 1) * P], gate_t_bf[:, c * BANK:(c + 1) * BANK],
                              start=True, stop=True).then_inc(wide_ready, 1)

                first(0)
                first(1)
                pe.wait_ge(gates_done, b + 1)
                for t in range(TILES):
                    mm = pe.matmul(ps[0:3 * EXPERTS, 4 + t // 4, (t % 4) * P:(t % 4 + 1) * P],
                                   gate3[:, t, :, :].rearrange("p a b -> p (a b)"), ident[:, :], start=True, stop=True)
                mm.then_inc(gates_turned, 1)
                pe.wait_ge(gates_copied, b * 2 + 2)
                wide(0)
                for m in range(FFN_STEPS):
                    c, n = divmod(m, SLICES)
                    if n == 0:
                        pe.matmul(ps[:, 6 + c, :], bias_rows[:, :], gate_t[:, c * BANK:(c + 1) * BANK],
                                  start=True, stop=False)
                    if m % 2 == 0 and m // 2 + 1 < WIDES:
                        wide(m // 2 + 1)
                    if m + 2 < FFN_STEPS:
                        first(m + 2)
                    pe.wait_ge(hidden_done, b * FFN_STEPS + m + 1)
                    pe.matmul(ps[:, 6 + c, :], w_out[:, n, :], hidden[:, m % 4, :], start=False,
                              stop=(n == SLICES - 1)).then_inc(hidden_used, 1)

        @block.scalar
        def _(act):
            with act.Fori(0, IMAGES // 2) as i:
                for j in range(2):
                    act.wait_ge(stats_done, i * 2 + j)
                    act.dma_start(x_in[:, j, :], a["x"][i * 2 + j]).then_inc(x_setup_in, 16)
            act.wait_ge(stats_done, IMAGES)
            act.dma_start(x_in[:, 0, :], a["x"][0]).then_inc(x_loaded, 16)
            act.wait_ge(setup_pe, 6)
            act.activation(se[0:SPLITS, 10, :], ps[0:SPLITS, 5, 0:IMAGES], ACT.Exp, scale=-1.0).then_inc(setup_act, 1)
            act.wait_ge(setup_pe, 7)
            act.activation(se[:, 11, :], ps[:, 6, 0:IMAGES], ACT.Exp, scale=-1.0).then_inc(setup_act, 1)
            act.wait_ge(setup_pool, 3)
            def image(b, last):
                act.wait_ge(back, b * 2 + 1)
                act.activation(norm_ch[:, :], flat(2), ACT.Copy).then_inc(norm_done, 1)
                for n, parts in enumerate((q_parts, k_parts)):
                    act.wait_ge(qk_ready, b * 2 + n + 1)
                    act.wait_ge(stack_in, b * STACK_INC)
                    act.activation(parts[:, 0, :], flat(4 + 2 * n), ACT.Copy).then_inc(qk_high, 1)
                for k in range(4):
                    act.wait_ge(vz_ready, b * 4 + k + 1)
                    pair = ps[:, k, :].rearrange("p (t w) -> p t w", t=2)
                    act.activation(v_aug[:, 2 * k:2 * k + 2, :, 0:DH],
                                   pair[:, :, 0:P].rearrange("p t (h d) -> p t h d", d=DH), ACT.Copy)
                    for t in range(2):
                        i = act.activation(z[:, 2 * k + t, :], pair[:, t, P:2 * P], ACT.Copy,
                                           scale=decay_norm[:, 2 * k + t:2 * k + t + 1])
                    i.then_inc(vz_done, 1)
                if not last:
                    act.wait_ge(x1_done, b + 1)
                    act.dma_start(x_in[:, 0, :], a["x"][b + 1]).then_inc(x_loaded, 16)
                for s in range(STEPS):
                    u, i = divmod(s, GROUP)
                    act.wait_ge(score_ready, b * STEPS + s + 1)
                    if u >= 2 and i == 0:
                        act.wait_ge(value_done, b * QUADS + u - 1)
                    act.activation(probs[:, u % 2, i, :], flat(2 * (s % 3)), ACT.Exp, scale=DH ** -0.5).then_inc(exp_done, 1)
                act.wait_ge(back, b * 2 + 2)
                act.activation(norm_ch[:, :], flat(2), ACT.Copy).then_inc(norm_done, 1)
                act.wait_ge(gap_done, b + 1)
                act.activation(gate_v[:, 3, :], gate_v[:, 2, :], ACT.Exp).then_inc(gap_exp, 1)
                act.wait_ge(gates_turned, b + 1)
                both = ps[0:3 * EXPERTS, 4:6, :].rearrange("p a b -> p (a b)")
                act.activation(gate_t[:, :], both, ACT.Copy).then_inc(gates_copied, 1)
                act.activation(gate_t_bf[:, :], both, ACT.Copy).then_inc(gates_copied, 1)
                for w in range(WIDES):
                    act.wait_ge(wide_ready, b * WIDES + w + 1)
                    if w >= 3:
                        act.wait_ge(hidden_done, b * FFN_STEPS + 2 * (w - 2))
                    act.activation(gate_wide[:, w % 3, :], ps[:, 4 + w % 2, :], ACT.Copy).then_inc(wide_done, 1)
                for c in range(HALVES):
                    act.wait_ge(result_done, b * HALVES + c + 1)
                    act.dma_start(out[b, :, c * BANK:(c + 1) * BANK],
                                  result[:, c * BANK:(c + 1) * BANK]).then_inc(stored, 16)

            with act.Fori(0, IMAGES - 1) as b:
                image(b, False)
            image(IMAGES - 1, True)
            act.wait_ge(stored, IMAGES * STORE_INC)

        @block.vector
        def _(dve):
            dve.wait_ge(const_in, CONST_INC)
            dve.tensor_copy(pick_bf[:, :], ttr_out[0:3 * EXPERTS, :]).then_inc(dot_done, 1)
            with dve.Fori(0, IMAGES // 2) as i:
                for j in range(2):
                    dve.wait_ge(x_setup_in, (i * 2 + j + 1) * 16)
                    dve.wait_ge(stats_done, i * 2 + j)
                    for c in range(HALVES):
                        last = dve.bn_stats(stat13[:, j, 6 * c:6 * c + 6], x_in[:, j, c * BANK:(c + 1) * BANK])
                    last.then_inc(bn_done, 1)
                    dve.wait_ge(dot_done, i * 2 + j + 1)
                    dve.tensor_tensor_reduce(ttr_out[:, :], x_in[:, j, :], dct[:, :], 1.0, 0.0, ALU.mult, ALU.add,
                                             stat13[:, j, 12:13]).then_inc(dot_done, 1)
                    dve.wait_ge(bn_done, i * 2 + j + 1)
                    dve.wait_ge(dot_done, i * 2 + j + 2)
                    dve.tensor_copy(stats[:, i * 2 + j, :], stat13[:, j, :]).then_inc(stats_done, 1)
            dve.wait_ge(stats_done, IMAGES)
            for n in range(IMAGES):
                last = dve.bn_aggr(moments[:, n, :], stats[:, n, 0:12])
            last.then_inc(aggr_done, 1)
            dve.wait_ge(aggr_done, 1)

            links = [0]

            def link(ins):
                links[0] += 1
                ins.then_inc(setup_chain, 1)
                dve.wait_ge(setup_chain, links[0])

            link(dve.memset(k_stack[SHIFT_ROW:STACK, :, :], 1.0))
            dve.tensor_copy(se[:, 0, :], moments[:, :, 0]).then_inc(setup_dve, 1)
            dve.wait_ge(setup_pe, 1)
            link(dve.tensor_copy(offset[:, :], ps[:, 0, 0:IMAGES]))
            link(dve.tensor_tensor(se[:, 1, :], se[:, 0, :], offset[:, :], ALU.subtract))
            link(dve.tensor_tensor(se[:, 1, :], se[:, 1, :], se[:, 1, :], ALU.mult))
            dve.tensor_tensor(se[:, 2, :], se[:, 1, :], moments[:, :, 1], ALU.add).then_inc(setup_dve, 1)
            dve.wait_ge(setup_pe, 2)
            dve.tensor_scalar(se[:, 3, :], ps[:, 1, 0:IMAGES], 1e-5, None, ALU.add).then_inc(setup_dve, 1)
            dve.wait_ge(setup_dve, 3)
            link(dve.tensor_scalar(se[:, 1, :], offset[:, :], dct_sum[:, 0:1], None, ALU.mult))
            link(dve.tensor_tensor(se[:, 1, :], stats[:, :, 12], se[:, 1, :], ALU.subtract))
            dve.wait_ge(setup_pool, 4)
            dve.tensor_tensor(se[:, 5, :], se[:, 1, :], se[:, 4, :], ALU.mult).then_inc(setup_dve, 1)
            dve.wait_ge(setup_pe, 3)
            dve.tensor_copy(se[0:SPLITS, 6, :], ps[0:SPLITS, 2, 0:IMAGES]).then_inc(setup_dve, 1)
            dve.wait_ge(setup_pe, 5)
            dve.tensor_scalar(se[0:SPLITS, 7, :], ps[0:SPLITS, 3, 0:IMAGES], 0.0, None, ALU.max).then_inc(setup_dve, 1)
            dve.tensor_scalar(se[0:SPLITS * HID, 8, :], ps[0:SPLITS * HID, 4, 0:IMAGES], 0.0, None,
                              ALU.max).then_inc(setup_dve, 1)
            dve.wait_ge(setup_act, 1)
            link(dve.tensor_scalar(se[0:SPLITS, 10, :], se[0:SPLITS, 10, :], 1.0, None, ALU.add))
            dve.reciprocal(se[0:SPLITS, 9, :], se[0:SPLITS, 10, :]).then_inc(setup_dve, 1)
            dve.wait_ge(setup_act, 2)
            link(dve.tensor_scalar(se[:, 11, :], se[:, 11, :], 1.0, None, ALU.add))
            link(dve.reciprocal(se[:, 11, :], se[:, 11, :]))
            dve.wait_ge(setup_pe, 8)
            link(dve.tensor_tensor(se[:, 1, :], se[:, 11, :], ps[:, 7, 0:IMAGES], ALU.mult))
            link(dve.tensor_tensor(se[:, 2, :], se[:, 1, :], se[:, 4, :], ALU.mult))
            link(dve.tensor_scalar(slope[:, :], se[:, 2, :], 1.0, None, ALU.add))
            link(dve.scalar_tensor_tensor(offset[:, :], se[:, 2, :], -1.0, offset[:, :], ALU.mult, ALU.mult))
            dve.wait_ge(setup_pe, 9)
            dve.tensor_copy(wvz[:, P:2 * P], ps[:, 0, 0:P]).then_inc(setup_dve, 1)
            dve.wait_ge(setup_pe, 10)
            for r in range(3):
                last = dve.tensor_tensor(bias3[:, r, :], b2_t[:, :], ps[:, 1, 0:EXPERTS], ALU.add)
            last.then_inc(setup_dve, 1)
            link(dve.tensor_scalar(neg_b1[:, :], b1[:, :], -1.0, None, ALU.mult))
            dve.wait_ge(setup_pe, 11)
            link(dve.tensor_copy(bias_rows[:, :], ps[0:3 * EXPERTS, 2, 0:P]))
            dve.sem_inc(setup_done, 1)

            def layer_norm(b, k):
                base = (b * 2 + k) * NORM_CHAIN
                dve.wait_ge(turned, b * 2 + k + 1)
                for t in range(TILES):
                    last = dve.bn_stats(norm6[:, t, :], tiles(0)[:, t, :])
                last.then_inc(dve_bn, 1)
                dve.wait_ge(dve_bn, b * 2 + k + 1)
                even, odd, s_even, s_odd = (norm6[:, :, c] for c in (1, 4, 2, 5))
                dve.tensor_tensor(norm_v[:, 0, :], even, odd, ALU.add)
                dve.tensor_tensor(norm_v[:, 1, :], even, odd, ALU.subtract)
                dve.tensor_tensor(norm_v[:, 2, :], s_even, s_odd, ALU.add).then_inc(dve_norm, 1)
                dve.wait_ge(dve_norm, base + 1)
                dve.tensor_scalar(norm_v[:, 3, :], norm_v[:, 0, :], 0.5, None, ALU.mult)
                dve.tensor_tensor(norm_v[:, 4, :], norm_v[:, 1, :], norm_v[:, 1, :], ALU.mult).then_inc(dve_norm, 1)
                dve.wait_ge(dve_norm, base + 2)
                dve.scalar_tensor_tensor(norm_v[:, 5, :], norm_v[:, 4, :], P / 4.0, norm_v[:, 2, :], ALU.mult,
                                         ALU.add).then_inc(dve_norm, 1)
                dve.wait_ge(dve_norm, base + 3)
                dve.tensor_scalar(norm_v[:, 6, :], norm_v[:, 5, :], 1.0 / P, 1e-5, ALU.mult,
                                  ALU.add).then_inc(dve_norm, 1)
                dve.wait_ge(rs_done, b * 2 + k + 1)
                for t in range(TILES):
                    last = dve.tensor_scalar(norm_tok[:, t, :], tiles(0)[:, t, :], norm_v[:, 3, t:t + 1],
                                             norm_rs[:, t:t + 1], ALU.subtract, ALU.mult)
                last.then_inc(tok_done, 1)

            with dve.Fori(0, IMAGES) as b:
                dve.wait_ge(x_loaded, (b + 1) * 16)
                dve.wait_ge(result_done, b * HALVES)
                dve.tensor_scalar(x1[:, :], x_in[:, 0, :], slope[:, bass.ds(b, 1)], offset[:, bass.ds(b, 1)],
                                  ALU.mult, ALU.add).then_inc(x1_done, 1)
                layer_norm(b, 0)
                for n, parts in enumerate((q_parts, k_parts)):
                    base = (b * 2 + n) * SPLIT_CHAIN
                    dve.wait_ge(qk_high, b * 2 + n + 1)
                    dve.wait_ge(qk_split, b * 2 + n)
                    dve.tensor_tensor(rest[:, :], flat(4 + 2 * n), parts[:, 0, :], ALU.subtract).then_inc(dve_split, 1)
                    dve.wait_ge(dve_split, base + 1)
                    dve.tensor_copy(parts[:, 1, :], rest[:, :]).then_inc(dve_split, 1)
                    dve.wait_ge(dve_split, base + 2)
                    dve.tensor_tensor(parts[:, 2, :], rest[:, :], parts[:, 1, :], ALU.subtract).then_inc(qk_split, 1)
                for n in range(STEPS):
                    dve.wait_ge(full_ready, b * STEPS + n + 1)
                    dve.tensor_reduce(row_max[:, n:n + 1], banks(2 * (n % 4), 2), AX.XY, ALU.max).then_inc(max_done, 1)
                turned_max = ps[0:STEPS, 0, 0:P]
                dve.wait_ge(max_turned, b + 1)
                dve.wait_ge(shift_in, b * SHIFT_INC)
                dve.tensor_scalar(max_parts[:, 0, :], turned_max, -1.0, None, ALU.mult).then_inc(dve_max, 1)
                dve.wait_ge(dve_max, b * MAX_CHAIN + 1)
                dve.scalar_tensor_tensor(max_rest[:, :], turned_max, -1.0, max_parts[:, 0, :], ALU.mult,
                                         ALU.subtract).then_inc(dve_max, 1)
                dve.wait_ge(dve_max, b * MAX_CHAIN + 2)
                dve.tensor_copy(max_parts[:, 1, :], max_rest[:, :]).then_inc(dve_mid, 1)
                dve.wait_ge(dve_mid, b + 1)
                dve.tensor_tensor(max_parts[:, 2, :], max_rest[:, :], max_parts[:, 1, :],
                                  ALU.subtract).then_inc(max_split, 1)
                for g in range(GROUPS):
                    dve.wait_ge(value_done, b * QUADS + (g + 1) * TILES)
                    dve.tensor_copy(o_sb[:, g, :], flat(6)).then_inc(o_copied, 1)
                for g in range(GROUPS):
                    dve.wait_ge(sums_wide, b * GROUPS + g + 1)
                    dve.wait_ge(o_scaled, b * GROUPS + g)
                    dve.reciprocal(rest[:, :], flat(2 * g)).then_inc(dve_o, 1)
                    dve.wait_ge(dve_o, b * GROUPS + g + 1)
                    dve.wait_ge(o_copied, b * GROUPS + g + 1)
                    dve.tensor_tensor(o_sb[:, g, :], o_sb[:, g, :], rest[:, :], ALU.mult).then_inc(o_scaled, 1)
                dve.wait_ge(attn_ready, b + 1)
                dve.scalar_tensor_tensor(t2[:, :], flat(6), b_out[:, 0:1], x1[:, :], ALU.add,
                                         ALU.add).then_inc(t2_done, 1)
                layer_norm(b, 1)

                dve.wait_ge(logits_ready, b + 1)
                steps = [0]

                def then(ins, go=True):
                    steps[0] += 1
                    ins.then_inc(dve_gate, 1)
                    if go:
                        dve.wait_ge(dve_gate, b * GATE_CHAIN + steps[0])

                def by_expert(ap):
                    return ap.rearrange("p (t e) -> p t e", e=EXPERTS)

                def wide(ap):
                    return ap.unsqueeze(2).broadcast_to([P, TILES, EXPERTS])

                logits, is_best, score, rest_l = gate[:, 0, :], gate[:, 1, :], gate[:, 2, :], gate[:, 3, :]
                best, top, gap, weight = gate_v[:, 0, :], gate_v[:, 1, :], gate_v[:, 2, :], gate_v[:, 3, :]
                then(dve.tensor_tensor(logits, ps[:, 4, 0:TILES * EXPERTS], b_gate[:, :], ALU.add))
                then(dve.tensor_reduce(best, by_expert(logits), AX.X, ALU.max))
                chosen = []
                for k in range(2):
                    src = logits if k == 0 else rest_l
                    value = best if k == 0 else gap
                    pick = gate[:, 4 + k, :]
                    then(dve.tensor_tensor(by_expert(is_best), by_expert(src), wide(value), ALU.is_equal))
                    then(dve.tensor_tensor(score, is_best, rank[:, :], ALU.mult))
                    then(dve.tensor_reduce(top, by_expert(score), AX.X, ALU.max))
                    then(dve.tensor_tensor(by_expert(pick), by_expert(rank[:, :]), wide(top), ALU.is_equal))
                    if k == 0:
                        then(dve.scalar_tensor_tensor(rest_l, pick, -3.0e38, logits, ALU.mult, ALU.add))
                        then(dve.tensor_reduce(gap, by_expert(rest_l), AX.X, ALU.max))
                dve.tensor_tensor(gate_v[:, 2, :], gap, best, ALU.subtract).then_inc(gap_done, 1)
                dve.wait_ge(gap_exp, b + 1)
                then(dve.tensor_scalar(gate_v[:, 4, :], weight, 1.0, None, ALU.add))
                then(dve.reciprocal(gate_v[:, 5, :], gate_v[:, 4, :]))
                then(dve.tensor_tensor(gate_v[:, 6, :], weight, gate_v[:, 5, :], ALU.mult))
                then(dve.tensor_tensor(by_expert(gate[:, 6, :]), by_expert(gate[:, 4, :]), wide(gate_v[:, 5, :]), ALU.mult),
                     go=False)
                then(dve.tensor_tensor(by_expert(gate[:, 7, :]), by_expert(gate[:, 5, :]), wide(gate_v[:, 6, :]), ALU.mult))
                then(dve.tensor_tensor(gate[:, 0, :], gate[:, 6, :], gate[:, 7, :], ALU.add))
                dve.wait_ge(gates_turned, b)
                for r in range(2):
                    then(dve.tensor_copy(gate_bf[:, :], gate[:, r, :]))
                    then(dve.tensor_copy(gate3[:, :, r, :], by_expert(gate_bf[:, :])), go=False)
                    then(dve.tensor_tensor(gate[:, r + 1, :], gate[:, r, :], gate_bf[:, :], ALU.subtract))
                dve.tensor_copy(gate3[:, :, 2, :], by_expert(gate[:, 2, :])).then_inc(gates_done, 1)
                assert steps[0] == GATE_CHAIN, steps[0]

                for m in range(FFN_STEPS):
                    c, n = divmod(m, SLICES)
                    dve.wait_ge(hidden_ready, b * FFN_STEPS + m + 1)
                    dve.wait_ge(wide_done, b * WIDES + m // FT + 1)
                    if m >= 4:
                        dve.wait_ge(hidden_used, b * FFN_STEPS + m - 3)
                    dve.scalar_tensor_tensor(hidden[:, m % 4, :], ps[:, m % 4, :], neg_b1[:, n:n + 1],
                                             gate_wide[:, (m // FT) % 3, :], ALU.max, ALU.mult).then_inc(hidden_done, 1)
                    if n == SLICES - 1:
                        at = slice(c * BANK, (c + 1) * BANK)
                        dve.wait_ge(hidden_used, b * FFN_STEPS + m + 1)
                        if c == 0:
                            dve.wait_ge(stored, b * STORE_INC)
                        dve.tensor_tensor(result[:, at], t2[:, at], ps[:, 6 + c, :], ALU.add).then_inc(result_done, 1)


_NAMES = ["L0_conv_W1", "L0_conv_W2", "L0_conv_M1", "L0_conv_M2", "L1_attn_W_qkv", "L1_attn_W_out",
          "L1_attn_b_out", "L1_ffn_w1", "L1_ffn_b1", "L1_ffn_w2", "L1_ffn_b2", "L1_ffn_wg", "L1_ffn_bg"]


def laid_out(x, w):
    c = np.ascontiguousarray
    qkvt, out = w["L1_attn_W_qkv"], w["L1_attn_W_out"].reshape(HEADS, 2, DH, P)
    w1_blocks = np.zeros((P, SPLITS * HID), np.float32)
    w2_blocks = np.zeros((SPLITS * HID, P), np.float32)
    wo1 = np.zeros((P, GROUPS, P), np.float32)
    for g in range(SPLITS):
        w1_blocks[g * CP_SPLIT:(g + 1) * CP_SPLIT, g * HID:(g + 1) * HID] = w["L0_conv_W1"][g].T
        w2_blocks[g * HID:(g + 1) * HID, g * CP_SPLIT:(g + 1) * CP_SPLIT] = w["L0_conv_W2"][g].T
    for h in range(HEADS):
        wo1[32 * (h % GROUP):32 * (h % GROUP) + DH, h // GROUP] = out[h, 0]
    return {
        "x": c(x.reshape(IMAGES, P, TOK)),
        "m1_t": c(w["L0_conv_M1"].T), "m2_t": c(w["L0_conv_M2"].T),
        "w1_blocks": w1_blocks, "w2_blocks": w2_blocks, "wo1": wo1,
        "wq": c(qkvt[:, 0:P]), "wk": c(qkvt[:, P:2 * P]), "wv": c(qkvt[:, 2 * P:3 * P]),
        "wt_t": c(qkvt[:, 3 * P:4 * P].T), "wo2": c(out[:, 1].reshape(P, P)),
        "b_out": c(w["L1_attn_b_out"].reshape(P, 1)),
        "w_in": c(w["L1_ffn_w1"].reshape(EXPERTS, P, FT, P).transpose(1, 0, 2, 3).reshape(P, SLICES, P)),
        "w_out": c(w["L1_ffn_w2"].reshape(EXPERTS, FT, P, P).transpose(2, 0, 1, 3).reshape(P, SLICES, P)),
        "b1": c(w["L1_ffn_b1"].reshape(SLICES, P).T), "b2_t": c(w["L1_ffn_b2"].T),
        "w_gate": c(w["L1_ffn_wg"]), "b_gate": c(np.broadcast_to(w["L1_ffn_bg"], (TILES, EXPERTS))),
    }


def kernel(**inputs):
    import concourse.bacc as bacc
    from concourse.bass_utils import run_bass_kernel_spmd

    x = np.asarray(inputs["x"])
    arrays = laid_out(x, {n: np.asarray(inputs[n]) for n in _NAMES})
    arrays.update(shape_constants())
    nc = bacc.Bacc("TRN2", target_bir_lowering=False, num_devices=1)
    a = {n: nc.dram_tensor(f"in_{n}", v.shape, F32, kind="ExternalInput").ap() for n, v in arrays.items()}
    out = nc.dram_tensor("out", (IMAGES, P, TOK), F32, kind="ExternalOutput").ap()
    build(nc, a, out)
    r = run_bass_kernel_spmd(nc, [{f"in_{n}": v for n, v in arrays.items()}], core_ids=[0])
    return r.results[0]["out"].reshape(x.shape)
```

```python
from contextlib import ExitStack

import numpy as np

import concourse.bass as bass
from concourse import mybir

F32 = mybir.dt.float32
BF16 = mybir.dt.bfloat16
F32R = mybir.dt.float32r
ALU = mybir.AluOpType
ACT = mybir.ActivationFunctionType
AX = mybir.AxisListType

P = 128
IMAGES = 16
SIDE = 32
TOK = SIDE * SIDE
TILES = TOK // P
BANK = 512
HALVES = TOK // BANK
HEADS, DH = 8, 16
GROUP = 4
GROUPS = HEADS // GROUP
SPLITS = 8
CP_SPLIT = P // SPLITS
HID = P // 16
NORM_GROUP = 4
EXPERTS, FF = 8, 256
FT = FF // P
SLICES = EXPERTS * FT
REACH = 2
STRIP = (2 * REACH + 1) * P
Q_PARTS = (0, 0, 0, 1, 1, 2)
K_PARTS = (0, 1, 2, 0, 1, 0)
PAIRS = len(Q_PARTS)
SHIFT_ROW = PAIRS * DH
STACK = SHIFT_ROW + 3
STEPS = HEADS * TILES
QUADS = GROUPS * TILES
GROUP_ROWS = GROUP * TILES
FFN_STEPS = HALVES * SLICES
WIDES = HALVES * EXPERTS
AHEAD = 3
HID_BUFS, PART_BUFS, WIDE_BUFS = 5, 3, 3
ROWS_INC = PAIRS * 16
STACK_INC = 2 * 16
SHIFT_INC = 3 * 16
STORE_INC = HALVES * 16
VALUES_INC = QUADS - GROUPS
NORM_CHAIN, SPLIT_CHAIN, MAX_CHAIN, GATE_CHAIN = 4, 2, 3, 24
MAX_SECOND = tuple(range(44, 64))
AT_SHIFT2 = 20
AT_BACK2, AT_LOGITS, AT_GATES = 22, 24, 32
GAP_LAG = 4
AT_COPY_O = (33, 35)
AT_FIRST, IN_SCORES = 38, 25
MAX_TAIL = {m: IN_SCORES + m for m in range(GROUP_ROWS - IN_SCORES)}
AT_SHIFT1 = 7
MAX_AFTER_PREP = 36
MAX_EARLY = {9: (32,), 10: (33,), 11: (34,), 12: (35,)}
MAX_EARLY.update({24 + k: (MAX_AFTER_PREP + k,) for k in range(8)})
AT_TURN_O, AT_BACK_O = (1, 3), 5
DECAY_TILES = {6: (0, 1), 7: (2, 3), 8: (4, 5), 9: (6, 7)}
AT_OUT, AT_RESIDUAL, AT_TURN_T2, AT_NORM2 = 10, 4, 12, 15
AT_VZ = (13, 15)
AT_AFFINE, AT_TURN_X, AT_NORM1, AT_BACK1, AT_Q, AT_K = 6, 17, 20, 21, 22, 23
DCT_X = (0, 0, 1, -1, 0, 3, 0, 2)
DCT_Y = (0, 1, 0, -1, 3, 0, 2, 0)


def shape_constants():
    def basis(freq):
        r = np.cos(np.pi * freq * (np.arange(SIDE) + 0.5) / SIDE) / np.sqrt(SIDE)
        return r * np.sqrt(2.0) if freq != 0 else r

    c = {}
    dct = np.zeros((P, SIDE, SIDE), np.float32)
    for i, (u, v) in enumerate(zip(DCT_X, DCT_Y)):
        dct[i * CP_SPLIT:(i + 1) * CP_SPLIT] = np.outer(basis(u), basis(v)).astype(np.float32)
    c["dct"] = dct.reshape(P, TOK)
    c["dct_sum"] = dct.astype(np.float64).sum((1, 2)).astype(np.float32).reshape(P, 1)
    ch = np.arange(P)
    c["ident"] = np.eye(P, dtype=np.float32)
    c["group_mean"] = (ch[:, None] // NORM_GROUP == ch[None] // NORM_GROUP).astype(np.float32) / NORM_GROUP
    member = (ch[:, None] // CP_SPLIT == np.arange(SPLITS)[None]).astype(np.float32)
    c["split_mean"] = member / CP_SPLIT
    c["split_spread"] = np.ascontiguousarray(member.T)
    dist = np.abs(np.arange(STRIP)[None] - REACH * P - ch[:, None]).astype(np.float32)
    c["decay"] = np.exp(-dist / np.float32(np.e)).astype(np.float32)
    pos = np.arange(TOK, dtype=np.float32)
    full = np.exp(-np.abs(pos[None] - pos[:, None]) / np.float32(np.e)).astype(np.float32)
    c["decay_norm"] = np.ascontiguousarray((1.0 / full.sum(-1)).astype(np.float32).reshape(TILES, P).T)
    pick = np.zeros((3, EXPERTS, EXPERTS, P), np.float32)
    for e in range(EXPERTS):
        pick[:, e, e] = 1.0
    c["gate_pick"] = pick.reshape(3 * EXPERTS, EXPERTS * P)
    c["rank"] = np.tile((EXPERTS - np.arange(EXPERTS)).astype(np.float32), (P, TILES))
    return {k: np.ascontiguousarray(v, dtype=np.float32) for k, v in c.items()}


def build(nc, a, out):
    nc.disable_value_cache = True
    with ExitStack() as ctx:
        def sb(name, shape, dt=F32):
            return ctx.enter_context(nc.sbuf_tensor(name, shape, dt))

        def sem(name):
            return ctx.enter_context(nc.semaphore(name))

        dct_sum = sb("dct_sum", [P, 1])
        ident = sb("ident", [P, P])
        split_mean = sb("split_mean", [P, SPLITS])
        split_spread = sb("split_spread", [SPLITS, P])
        decay = sb("decay", [P, STRIP])
        decay_norm = sb("decay_norm", [P, TILES])
        rank = sb("rank", [P, TILES * EXPERTS])
        pick_bf = sb("pick_bf", [3 * EXPERTS, EXPERTS * P], BF16)
        m1_t = sb("m1_t", [SPLITS, SPLITS])
        m2_t = sb("m2_t", [SPLITS, SPLITS])
        wq = sb("wq", [P, P])
        wk = sb("wk", [P, P])
        wvz = sb("wvz", [P, 2 * P])
        wo1 = sb("wo1", [P, P])
        b_out = sb("b_out", [P, 1])
        w_in = sb("w_in", [P, 2, SLICES, P], F32R)
        w_out = sb("w_out", [P, 2, SLICES, P], F32R)
        b1 = sb("b1", [P, SLICES])
        neg_b1 = sb("neg_b1", [P, SLICES])
        b2_t = sb("b2_t", [P, EXPERTS])
        w_gate = sb("w_gate", [P, EXPERTS])
        b_gate = sb("b_gate", [P, TILES * EXPERTS])
        bias3 = sb("bias3", [P, 3, EXPERTS])
        bias_rows = sb("bias_rows", [3 * EXPERTS, P])
        minus_half = sb("minus_half", [P, IMAGES])
        zero = sb("zero", [P, 1])

        stat13 = sb("stat13", [P, 2, 13])
        moments = sb("moments", [P, IMAGES, 2])
        stats = sb("stats", [P, IMAGES, 13])
        se = sb("se", [P, 12, IMAGES])
        slope = sb("slope", [P, IMAGES])
        offset = sb("offset", [P, IMAGES])

        x_in = sb("x_in", [P, 2, TOK])
        norm6 = sb("norm6", [P, 2, TILES, 6])
        norm_v = sb("norm_v", [P, 2, 7, TILES])
        norm_rs = sb("norm_rs", [P, 2, TILES])
        norm_tok = sb("norm_tok", [P, 2, TILES, P])
        on_tok = norm_tok[:, 0, :, :]
        norm_ch = sb("norm_ch", [P, TOK])
        q_parts = sb("q_parts", [P, 3, TOK], BF16)
        k_parts = sb("k_parts", [P, 3, TOK], BF16)
        rest = sb("rest", [P, TOK])
        on_ch = rest
        q_stack = sb("q_stack", [STACK, HEADS, TOK], BF16)
        k_stack = sb("k_stack", [STACK, HEADS, TOK], BF16)
        v_aug = sb("v_aug", [P, TILES, HEADS, 32])
        z = sb("z", [P, TILES, P])
        half_max = sb("half_max", [P, HALVES, STEPS])
        row_max = sb("row_max", [P, STEPS])
        max_parts = sb("max_parts", [GROUP_ROWS, 3, P], BF16)
        max_rest = sb("max_rest", [GROUP_ROWS, P])
        o_sb = (rest[:, :], k_parts[:, 0:2, :].rearrange("p a b -> p (a b)").bitcast(F32))
        o_recip = sb("o_recip", [P, GROUPS, TILES, GROUP])
        t2 = sb("t2", [P, TOK])
        t2_next = x_in[:, 1, :]
        n2 = sb("n2", [P, 2, TOK], F32R)
        gate = sb("gate", [P, 8, TILES * EXPERTS])
        gate_v = sb("gate_v", [P, 8, TILES])
        gate_bf = sb("gate_bf", [P, TILES * EXPERTS], BF16)
        gate3 = sb("gate3", [P, TILES, 3, EXPERTS])
        gate_t = sb("gate_t", [3 * EXPERTS, TOK])
        gate_t_bf = sb("gate_t_bf", [3 * EXPERTS, TOK], BF16)

        region = sb("region", [P, 2 * GROUP * TOK])
        taken = [0]

        def part(cols, rows=P):
            taken[0] += cols
            assert taken[0] <= 2 * GROUP * TOK
            return region[0:rows, taken[0] - cols:taken[0]]

        w_in_raw, w_out_raw = part(SLICES * P), part(SLICES * P)
        dct, dot_out, picks = part(TOK), part(TOK), part(TOK, 3 * EXPERTS)
        group_mean, wt_t, wo2 = part(P), part(P), part(P)
        w1_blocks, w2_blocks = part(SPLITS * HID), part(P, SPLITS * HID)
        probs = region[:, :].rearrange("p (u i t) -> p u i t", u=2, i=GROUP)
        taken[0] = 0
        hidden = [part(BANK) for _ in range(HID_BUFS)]
        gate_wide = [part(BANK) for _ in range(WIDE_BUFS)]

        hid_parts = sb("hid_parts", [P, 2, PART_BUFS, BANK], F32R)
        hid_high = [hid_parts[:, 0, k, :] for k in range(PART_BUFS)]
        hid_low = [hid_parts[:, 1, k, :] for k in range(PART_BUFS)]

        ps = ctx.enter_context(nc.psum_tensor("ps", [P, 8, BANK], F32))
        SIDE_A, SIDE_B, O_BANKS = 4, 6, 6
        CB, YB = 2, 3

        q_rows = nc.dram_tensor("q_rows", (PAIRS, P, TOK), BF16, kind="Internal").ap()
        k_rows = nc.dram_tensor("k_rows", (PAIRS, P, TOK), BF16, kind="Internal").ap()

        const_in = sem("const_in")
        x_setup_in = sem("x_setup_in")
        stats_done = sem("stats_done")
        setup_pe = sem("setup_pe")
        setup_dve = sem("setup_dve")
        setup_act = sem("setup_act")
        setup_pool = sem("setup_pool")
        setup_chain = sem("setup_chain")
        setup_done = sem("setup_done")
        bn_done = sem("bn_done")
        dot_done = sem("dot_done")
        aggr_done = sem("aggr_done")
        x_next_in = sem("x_next_in")
        x_now_in = sem("x_now_in")
        x1_done = sem("x1_done")
        res_done = sem("res_done")
        turned = [sem(f"turned{k}") for k in (1, 2)]
        bn_taken = [sem(f"bn_taken{k}") for k in (1, 2)]
        norm_step = [sem(f"norm_step{k}") for k in (1, 2)]
        rs_done = [sem(f"rs_done{k}") for k in (1, 2)]
        tok_done = [sem(f"tok_done{k}") for k in (1, 2)]
        back = [sem(f"back{k}") for k in (1, 2)]
        norm_done = sem("norm_done")
        n2_high = sem("n2_high")
        n2_done = sem("n2_done")
        q_ready = sem("q_ready")
        k_ready = sem("k_ready")
        q_high = sem("q_high")
        k_high = sem("k_high")
        qk_split = sem("qk_split")
        dve_split = sem("dve_split")
        rows_out = sem("rows_out")
        stack_in = [sem(f"stack_in{p}") for p in range(HEADS // 2)]
        vz_ready = sem("vz_ready")
        vz_done = sem("vz_done")
        full_ready = sem("full_ready")
        max_done = sem("max_done")
        max_joined = sem("max_joined")
        max_turned = sem("max_turned")
        max_step = sem("max_step")
        max_split = sem("max_split")
        shift_in = sem("shift_in")
        score_ready = sem("score_ready")
        exp_done = sem("exp_done")
        value_done = sem("value_done")
        half_done = sem("half_done")
        o_copied = sem("o_copied")
        o_turned = sem("o_turned")
        recip_done = sem("recip_done")
        o_scaled = sem("o_scaled")
        on_back = sem("on_back")
        on_done = sem("on_done")
        attn_ready = sem("attn_ready")
        t2_done = sem("t2_done")
        t2_copied = sem("t2_copied")
        logits_ready = sem("logits_ready")
        gate_step = sem("gate_step")
        gap_done = sem("gap_done")
        gap_exp = sem("gap_exp")
        gates_done = sem("gates_done")
        gates_turned = sem("gates_turned")
        gates_copied = sem("gates_copied")
        wide_ready = sem("wide_ready")
        wide_done = sem("wide_done")
        hidden_ready = sem("hidden_ready")
        hidden_done = sem("hidden_done")
        high_done = sem("high_done")
        low_done = sem("low_done")
        hidden_used = sem("hidden_used")
        result_done = sem("result_done")
        stored = sem("stored")

        consts = [(dct, "dct"), (dct_sum[:, :], "dct_sum"), (ident[:, :], "ident"), (group_mean, "group_mean"),
                  (split_mean[:, :], "split_mean"), (split_spread[:, :], "split_spread"),
                  (decay[:, :], "decay"), (decay_norm[:, :], "decay_norm"), (rank[:, :], "rank"),
                  (m1_t[:, :], "m1_t"), (m2_t[:, :], "m2_t"), (w1_blocks, "w1_blocks"), (w2_blocks, "w2_blocks"),
                  (wq[:, :], "wq"), (wk[:, :], "wk"), (wvz[:, 0:P], "wv"), (wo1[:, :], "wo1"), (wt_t, "wt_t"),
                  (wo2, "wo2"), (b_out[:, :], "b_out"), (b1[:, :], "b1"), (b2_t[:, :], "b2_t"),
                  (w_gate[:, :], "w_gate"), (picks, "gate_pick"), (w_in_raw, "w_in"), (w_out_raw, "w_out"),
                  (b_gate[:, :].rearrange("p (t e) -> p t e", t=TILES), "b_gate")]
        CONST_INC = 16 * len(consts)

        def flat(lo):
            return ps[:, lo:lo + 2, :].rearrange("p a b -> p (a b)")

        def tiles(lo):
            return ps[:, lo:lo + 2, :].rearrange("p a (b c) -> p (a b) c", c=P)

        block = ctx.enter_context(nc.Block())

        @block.sync
        def _(sp):
            for tile, name in consts:
                src = a[name]
                if name == "b_gate":
                    src = src.unsqueeze(0).broadcast_to([P, TILES, EXPERTS])
                sp.dma_start(tile, src).then_inc(const_in, 16)

            def rows_to_dram(q_split, k_split, spent):
                sp.wait_ge(qk_split, q_split)
                if spent is not None:
                    for p in range(HEADS // 2):
                        sp.wait_ge(stack_in[p], spent)
                sp.dma_start(q_rows[0:3].rearrange("s p t -> p s t"),
                             q_parts[:, 0:1, :].broadcast_to([P, 3, TOK])).then_inc(rows_out, 16)
                sp.dma_start(q_rows[3:5].rearrange("s p t -> p s t"),
                             q_parts[:, 1:2, :].broadcast_to([P, 2, TOK])).then_inc(rows_out, 16)
                sp.dma_start(q_rows[5], q_parts[:, 2, :]).then_inc(rows_out, 16)
                sp.wait_ge(qk_split, k_split)
                sp.dma_start(k_rows[0:3].rearrange("s p t -> p s t"), k_parts[:, 0:3, :]).then_inc(rows_out, 16)
                sp.dma_start(k_rows[3:5].rearrange("s p t -> p s t"), k_parts[:, 0:2, :]).then_inc(rows_out, 16)
                sp.dma_start(k_rows[5], k_parts[:, 0, :]).then_inc(rows_out, 16)

            def load_stacks(g):
                for p in range(2):
                    heads = slice(g * GROUP + 2 * p, g * GROUP + 2 * p + 2)
                    for stack, rows in ((q_stack, q_rows), (k_stack, k_rows)):
                        by_row = rows.rearrange("s (d h) t -> (s d) h t", h=HEADS)
                        sp.dma_start(stack[0:SHIFT_ROW, heads, :], by_row[:, heads, :]).then_inc(stack_in[2 * g + p], 16)

            def load_shift(g):
                for j in range(3):
                    sp.dma_start(q_stack[SHIFT_ROW + j:SHIFT_ROW + j + 1, g * GROUP:(g + 1) * GROUP, :]
                                 .rearrange("p h (t q) -> p (h t) q", q=P),
                                 max_parts[:, j, :]).then_inc(shift_in, 16)

            rows_to_dram(1, 2, None)
            sp.wait_ge(rows_out, ROWS_INC)
            load_stacks(0)
            load_stacks(1)
            rows_to_dram(3, 4, STACK_INC)
            sp.wait_ge(max_split, 1)
            load_shift(0)

            def image(i, nxt, prep):
                def count(each, more):
                    return i * each + more if isinstance(i, int) else sp.snap(i * each + more)

                second_max, first_max = count(2, 2), count(2, 3)
                middle, after = count(STEPS, STEPS // 2), count(STEPS, STEPS)
                written, loaded = count(ROWS_INC, 2 * ROWS_INC), count(STACK_INC, 2 * STACK_INC)
                q_split, k_split = count(2, 5), count(2, 6)
                sp.wait_ge(max_split, second_max)
                load_shift(1)
                if nxt:
                    sp.wait_ge(rows_out, written)
                    sp.wait_ge(score_ready, middle)
                    load_stacks(0)
                    sp.wait_ge(score_ready, after)
                    load_stacks(1)
                    sp.wait_ge(max_split, first_max)
                    load_shift(0)
                if prep:
                    rows_to_dram(q_split, k_split, loaded)

            image(0, True, True)
            with sp.Fori(1, IMAGES - 2) as i:
                image(i, True, True)
            image(IMAGES - 2, True, False)
            image(IMAGES - 1, False, False)
            sp.wait_ge(rows_out, IMAGES * ROWS_INC)

        @block.gpsimd
        def _(pool):
            pool.memset(minus_half[:, :], -0.5).then_inc(setup_pool, 1)
            pool.memset(v_aug[:, :, :, :], 0.0).then_inc(setup_pool, 1)
            pool.wait_ge(setup_pool, 2)
            pool.memset(v_aug[:, :, :, DH:DH + 1], 1.0).then_inc(setup_pool, 1)
            pool.memset(zero[:, :], 0.0)
            pool.wait_ge(setup_pool, 3)
            pool.wait_ge(setup_dve, 3)
            pool.tensor_tensor(se[:, 4, :], se[:, 3, :], minus_half[:, :], ALU.pow).then_inc(setup_pool, 1)

            def reciprocal_root(k, j):
                pool.wait_ge(norm_step[j], (k + 1) * NORM_CHAIN)
                pool.tensor_tensor(norm_rs[:, j, :], norm_v[:, j, 6, :], minus_half[:, 0:TILES],
                                   ALU.pow).then_inc(rs_done[j], 1)

            def low_part(j, m):
                pool.wait_ge(high_done, j * FFN_STEPS + m + 1)
                pool.tensor_tensor(hid_low[m % PART_BUFS], hidden[m % HID_BUFS],
                                   hid_high[m % PART_BUFS].bitcast(F32), ALU.subtract).then_inc(low_done, 1)

            def experts(i, j, ffn, nxt, prep):
                if ffn:
                    for m in range(AHEAD):
                        low_part(j, m)
                for m in range(FFN_STEPS):
                    if i is not None and m == AT_NORM2:
                        reciprocal_root(i, 1)
                    if prep and m == AT_NORM1:
                        reciprocal_root(i + 2, 0)
                    if ffn and m + AHEAD < FFN_STEPS:
                        low_part(j, m + AHEAD)
                if i is not None:
                    if ffn:
                        pool.wait_ge(stored, i * STORE_INC)
                    pool.wait_ge(t2_done, i + 1)
                    pool.tensor_tensor(t2[:, :], t2_next, zero[:, :].broadcast_to([P, TOK]), ALU.add).then_inc(t2_copied, 1)

            reciprocal_root(0, 0)
            reciprocal_root(1, 0)
            experts(0, None, False, True, True)
            with pool.Fori(1, IMAGES - 2) as i:
                experts(i, i - 1, True, True, True)
            experts(IMAGES - 2, IMAGES - 3, True, True, False)
            experts(IMAGES - 1, IMAGES - 2, True, False, False)
            experts(None, IMAGES - 1, True, False, False)

        @block.tensor
        def _(pe):
            def small(bank, rows, cols, lhs_t, rhs):
                return pe.matmul(ps[0:rows, bank, 0:cols], lhs_t, rhs, start=True, stop=True)

            pe.wait_ge(const_in, CONST_INC)
            pe.wait_ge(setup_dve, 1)
            small(0, P, IMAGES, group_mean, se[:, 0, :]).then_inc(setup_pe, 1)
            pe.wait_ge(setup_dve, 2)
            small(1, P, IMAGES, group_mean, se[:, 2, :]).then_inc(setup_pe, 1)
            pe.wait_ge(setup_dve, 4)
            small(2, SPLITS, IMAGES, split_mean[:, :], se[:, 5, :]).then_inc(setup_pe, 1)
            pe.wait_ge(setup_dve, 5)
            small(3, SPLITS, IMAGES, m1_t[:, :], se[0:SPLITS, 6, :]).then_inc(setup_pe, 1)
            small(4, SPLITS * HID, IMAGES, w1_blocks, se[:, 5, :]).then_inc(setup_pe, 1)
            pe.wait_ge(setup_dve, 6)
            small(5, SPLITS, IMAGES, m2_t[:, :], se[0:SPLITS, 7, :]).then_inc(setup_pe, 1)
            pe.wait_ge(setup_dve, 7)
            small(6, P, IMAGES, w2_blocks, se[0:SPLITS * HID, 8, :]).then_inc(setup_pe, 1)
            pe.wait_ge(setup_dve, 8)
            small(7, P, IMAGES, split_spread[:, :], se[0:SPLITS, 9, :]).then_inc(setup_pe, 1)
            small(0, P, P, wt_t, wo2).then_inc(setup_pe, 1)
            for e in range(EXPERTS):
                for f in range(FT):
                    n = e * FT + f
                    mm = pe.matmul(ps[:, 1, e:e + 1], w_out_raw[:, n * P:(n + 1) * P], b1[:, n:n + 1],
                                   start=(f == 0), stop=(f == FT - 1))
            mm.then_inc(setup_pe, 1)
            pe.wait_ge(setup_dve, 10)
            small(2, 3 * EXPERTS, P, bias3[:, :, :].rearrange("p a b -> p (a b)"), ident[:, :]).then_inc(setup_pe, 1)

            def turn_x(k):
                pe.wait_ge(x1_done, k + 1)
                for t in range(TILES):
                    mm = pe.transpose(tiles(SIDE_A)[:, t, :], x_in[:, 0, t * P:(t + 1) * P], ident[:, :])
                mm.then_inc(turned[0], 1)

            def turn_back_n1(k):
                pe.wait_ge(tok_done[0], k + 1)
                for t in range(TILES):
                    mm = pe.transpose(tiles(SIDE_A)[:, t, :], norm_tok[:, 0, t, :], ident[:, :])
                mm.then_inc(back[0], 1)

            def project(k, w, lo, ready):
                pe.wait_ge(norm_done, k + 1)
                for c in range(HALVES):
                    mm = pe.matmul(ps[:, lo + c, :], w[:, :], norm_ch[:, c * BANK:(c + 1) * BANK], start=True, stop=True)
                mm.then_inc(ready, 1)

            def values_and_z(k, r):
                if r:
                    pe.wait_ge(vz_done, k * 4 + 2)
                for t in range(4 * r, 4 * r + 4):
                    mm = pe.matmul(ps[:, SIDE_A + t // 2 % 2, (t % 2) * 2 * P:(t % 2 + 1) * 2 * P],
                                   norm_ch[:, t * P:(t + 1) * P], wvz[:, :], start=True, stop=True)
                    if t % 2:
                        mm.then_inc(vz_ready, 1)

            def full_scores(k, n):
                h, t = divmod(n, TILES)
                if n % (2 * TILES) == 0:
                    pe.wait_ge(stack_in[h // 2], k * STACK_INC + STACK_INC)
                for c in range(HALVES):
                    if n > 0:
                        pe.wait_ge(max_done, k * 2 * STEPS + 2 * n - 1 + c)
                    pe.matmul(ps[:, SIDE_A + c, :], q_stack[0:SHIFT_ROW, h, t * P:(t + 1) * P],
                              k_stack[0:SHIFT_ROW, h, c * BANK:(c + 1) * BANK], start=True,
                              stop=True).then_inc(full_ready, 1)

            def turn_maxima(k, g):
                pe.wait_ge(max_joined, k * 2 + g + 1)
                pe.matmul(ps[0:GROUP_ROWS, SIDE_A, 0:P], row_max[:, g * GROUP_ROWS:(g + 1) * GROUP_ROWS], ident[:, :],
                          start=True, stop=True).then_inc(max_turned, 1)

            def turn_back_n2(j):
                pe.wait_ge(tok_done[1], j + 1)
                for t in range(TILES):
                    mm = pe.transpose(tiles(SIDE_A)[:, t, :], norm_tok[:, 1, t, :], ident[:, :])
                mm.then_inc(back[1], 1)

            def gate_logits(j):
                pe.wait_ge(n2_done, j + 1)
                for t in range(TILES):
                    for part in range(2):
                        mm = pe.matmul(ps[:, SIDE_A, t * EXPERTS:(t + 1) * EXPERTS],
                                       n2[:, part, t * P:(t + 1) * P].bitcast(F32), w_gate[:, :],
                                       start=(part == 0), stop=(part == 1))
                mm.then_inc(logits_ready, 1)

            def turn_gates(j):
                pe.wait_ge(gates_done, j + 1)
                for t in range(TILES):
                    mm = pe.matmul(ps[0:3 * EXPERTS, SIDE_A + t // 4, (t % 4) * P:(t % 4 + 1) * P],
                                   gate3[:, t, :, :].rearrange("p a b -> p (a b)"), ident[:, :], start=True, stop=True)
                mm.then_inc(gates_turned, 1)

            def scores(i, s):
                g, r = divmod(s, TILES * GROUP)
                t, h = r // GROUP, g * GROUP + r % GROUP
                if s == 0:
                    pe.wait_ge(shift_in, i * 2 * SHIFT_INC + SHIFT_INC)
                if s == STEPS // 2:
                    pe.wait_ge(shift_in, i * 2 * SHIFT_INC + 2 * SHIFT_INC)
                for c in range(HALVES):
                    mm = pe.matmul(ps[:, 2 * (s % 2) + c, :], k_stack[:, h, t * P:(t + 1) * P],
                                   q_stack[:, h, c * BANK:(c + 1) * BANK], start=True, stop=True)
                mm.then_inc(score_ready, 1)

            def values(i, u, j):
                g, t = divmod(u, TILES)
                c, part = divmod(j, 2)
                if u == TILES and part == 0:
                    pe.wait_ge(o_copied, i * 4 + c + 1)
                at = slice(j * BANK // 2, (j + 1) * BANK // 2)
                for r in range(GROUP):
                    mm = pe.matmul(ps[32 * r:32 * r + 32, O_BANKS + c, part * BANK // 2:(part + 1) * BANK // 2],
                                   v_aug[:, t, g * GROUP + r, :], probs[:, u % 2, r, at],
                                   start=(t == 0 and part == 0), stop=(t == TILES - 1 and part == 1))
                if t == TILES - 1 and part == 1:
                    mm.then_inc(half_done, 1)
                if j == 3 and not (t == TILES - 1):
                    mm.then_inc(value_done, 1)

            def attention(i, j, ffn, nxt):
                pe.wait_ge(vz_done, i * 4 + 4)
                scores(i, 0)
                scores(i, 1)
                for s in range(STEPS):
                    if s + 2 < STEPS:
                        pe.wait_ge(exp_done, i * STEPS + s + 1)
                        scores(i, s + 2)
                    if s < len(MAX_SECOND):
                        full_scores(i, MAX_SECOND[s])
                    if s == AT_SHIFT2:
                        turn_maxima(i, 1)
                    if ffn and s == AT_BACK2:
                        pe.wait_ge(max_split, i * 2 + 2)
                        turn_back_n2(j)
                    if ffn and s == AT_LOGITS:
                        gate_logits(j)
                    if ffn and s == AT_GATES:
                        turn_gates(j)
                    if nxt and s == AT_FIRST:
                        pe.wait_ge(max_split, i * 2 + 2)
                        if ffn:
                            pe.wait_ge(gates_copied, j * 2 + 2)
                    if nxt and AT_FIRST <= s < AT_FIRST + IN_SCORES:
                        full_scores(i + 1, s - AT_FIRST)
                    if s >= 3:
                        if s == STEPS - 1:
                            pe.wait_ge(exp_done, i * STEPS + STEPS)
                        values(i, (s - 3) // GROUP, (s - 3) % GROUP)
                for s in range(STEPS, STEPS + 3):
                    values(i, (s - 3) // GROUP, (s - 3) % GROUP)

            def turn_o(i, g):
                if g == 0:
                    pe.wait_ge(o_copied, i * 4 + 4)
                else:
                    pe.wait_ge(o_scaled, i * 2 + 1)
                for t in range(TILES):
                    mm = pe.transpose(tiles(SIDE_B)[:, t, :], o_sb[g][:, t * P:(t + 1) * P], ident[:, :])
                mm.then_inc(o_turned, 1)

            def turn_back_o(i):
                pe.wait_ge(o_scaled, i * 2 + 2)
                for t in range(TILES):
                    mm = pe.transpose(tiles(SIDE_B)[:, t, :], on_tok[:, t, :], ident[:, :])
                mm.then_inc(on_back, 1)

            def decay_tile(i, t):
                if t == 0:
                    pe.wait_ge(on_done, i + 1)
                near = range(max(0, t - REACH), min(TILES, t + REACH + 1))
                for kt in near:
                    at = (t - kt + REACH) * P
                    pe.matmul(ps[:, SIDE_B + t // 4, (t % 4) * P:(t % 4 + 1) * P], z[:, kt, :], decay[:, at:at + P],
                              start=(t % 4 == 0 and kt == near[0]), stop=False)

            def project_out():
                for c in range(HALVES):
                    mm = pe.matmul(ps[:, SIDE_B + c, :], wo1[:, :], on_ch[:, c * BANK:(c + 1) * BANK],
                                   start=False, stop=True)
                mm.then_inc(attn_ready, 1)

            def turn_t2(i):
                pe.wait_ge(t2_done, i + 1)
                for t in range(TILES):
                    mm = pe.transpose(tiles(SIDE_B)[:, t, :], x_in[:, 1, t * P:(t + 1) * P], ident[:, :])
                mm.then_inc(turned[1], 1)

            def three_passes(bank, w, n, high, low, start, stop):
                pe.matmul(ps[:, bank, :], w[:, 0, n, :], high, start=start, stop=False)
                pe.matmul(ps[:, bank, :], w[:, 0, n, :], low, start=False, stop=False)
                return pe.matmul(ps[:, bank, :], w[:, 1, n, :], high, start=False, stop=stop)

            def first(j, m):
                c, n = divmod(m, SLICES)
                if m >= 2:
                    pe.wait_ge(hidden_done, j * FFN_STEPS + m - 1)
                at = slice(c * BANK, (c + 1) * BANK)
                three_passes(m % 2, w_in, n, n2[:, 0, at], n2[:, 1, at], True, True).then_inc(hidden_ready, 1)

            def second(j, m):
                c, n = divmod(m, SLICES)
                pe.wait_ge(low_done, j * FFN_STEPS + m + 1)
                three_passes(YB, w_out, n, hid_high[m % PART_BUFS], hid_low[m % PART_BUFS], False,
                             n == SLICES - 1).then_inc(hidden_used, 1)

            def wide(j, w):
                c, e = divmod(w, EXPERTS)
                if w >= 1:
                    pe.wait_ge(wide_done, j * WIDES + w)
                pe.matmul(ps[:, CB, :], pick_bf[:, e * P:(e + 1) * P], gate_t_bf[:, c * BANK:(c + 1) * BANK],
                          start=True, stop=True).then_inc(wide_ready, 1)

            def biases(j, c):
                if c:
                    pe.wait_ge(result_done, j * HALVES + 1)
                pe.matmul(ps[:, YB, :], bias_rows[:, :], gate_t[:, c * BANK:(c + 1) * BANK], start=True, stop=False)

            def experts(i, j, ffn, nxt, prep):
                if ffn:
                    pe.wait_ge(gates_copied, j * 2 + 2)
                    wide(j, 0)
                    first(j, 0)
                    first(j, 1)
                    wide(j, 1)
                    first(j, 2)
                    biases(j, 0)
                for m in range(FFN_STEPS):
                    if nxt and m in MAX_TAIL:
                        full_scores(i + 1, MAX_TAIL[m])
                    if nxt and m == AT_SHIFT1:
                        turn_maxima(i + 1, 0)
                    if nxt and m in MAX_EARLY:
                        if MAX_EARLY[m][0] == GROUP_ROWS:
                            pe.wait_ge(max_split, i * 2 + 3)
                        if MAX_EARLY[m][0] == MAX_AFTER_PREP:
                            if prep:
                                pe.wait_ge(qk_split, i * 2 + 5)
                            else:
                                pe.wait_ge(vz_done, i * 4 + 8)
                        for n in MAX_EARLY[m]:
                            full_scores(i + 1, n)
                    if i is not None:
                        if m in AT_TURN_O:
                            turn_o(i, AT_TURN_O.index(m))
                        if m == AT_BACK_O:
                            turn_back_o(i)
                        if m in DECAY_TILES:
                            for t in DECAY_TILES[m]:
                                decay_tile(i, t)
                        if m == AT_OUT:
                            project_out()
                        if m == AT_TURN_T2:
                            turn_t2(i)
                    if nxt and m == AT_VZ[0]:
                        pe.wait_ge(max_done, i * 2 * STEPS + 2 * STEPS + 2 * (MAX_AFTER_PREP - 1) + 2)
                        values_and_z(i + 1, 0)
                    if nxt and m == AT_VZ[1]:
                        values_and_z(i + 1, 1)
                    if prep:
                        if m == AT_TURN_X:
                            pe.wait_ge(vz_done, i * 4 + 8)
                            turn_x(i + 2)
                        if m == AT_BACK1:
                            turn_back_n1(i + 2)
                        if m == AT_Q:
                            project(i + 2, wq, SIDE_A, q_ready)
                        if m == AT_K:
                            pe.wait_ge(tok_done[1], i + 1)
                            project(i + 2, wk, SIDE_B, k_ready)
                    if ffn:
                        if m % 2 == 0 and m // 2 + 2 < WIDES:
                            wide(j, m // 2 + 2)
                        if m + AHEAD < FFN_STEPS:
                            first(j, m + AHEAD)
                        if m == SLICES:
                            biases(j, 1)
                        second(j, m)
                if ffn and i is not None:
                    pe.wait_ge(result_done, i * HALVES)
                if prep:
                    pe.wait_ge(qk_split, i * 2 + 6)
                if nxt and not prep:
                    pe.wait_ge(tok_done[1], i + 1)

            pe.wait_ge(setup_done, 1)
            pe.wait_ge(setup_pool, 3)
            turn_x(0)
            turn_back_n1(0)
            project(0, wq, SIDE_A, q_ready)
            project(0, wk, SIDE_B, k_ready)
            pe.wait_ge(qk_split, 1)
            values_and_z(0, 0)
            values_and_z(0, 1)
            pe.wait_ge(vz_done, 4)
            turn_x(1)
            turn_back_n1(1)
            project(1, wq, SIDE_A, q_ready)
            pe.wait_ge(qk_split, 2)
            project(1, wk, SIDE_B, k_ready)
            pe.wait_ge(qk_split, 4)
            pe.wait_ge(setup_done, 2)
            for n in range(GROUP_ROWS):
                full_scores(0, n)
            turn_maxima(0, 0)
            pe.wait_ge(max_split, 1)
            for n in range(GROUP_ROWS, MAX_SECOND[0]):
                full_scores(0, n)

            attention(0, None, False, True)
            experts(0, None, False, True, True)
            with pe.Fori(1, IMAGES - 2) as i:
                attention(i, i - 1, True, True)
                experts(i, i - 1, True, True, True)
            attention(IMAGES - 2, IMAGES - 3, True, True)
            experts(IMAGES - 2, IMAGES - 3, True, True, False)
            attention(IMAGES - 1, IMAGES - 2, True, False)
            experts(IMAGES - 1, IMAGES - 2, True, False, False)
            turn_back_n2(IMAGES - 1)
            gate_logits(IMAGES - 1)
            turn_gates(IMAGES - 1)
            experts(None, IMAGES - 1, True, False, False)

        @block.scalar
        def _(act):
            with act.Fori(0, IMAGES // 2) as i:
                for j in range(2):
                    act.wait_ge(stats_done, i * 2 + j)
                    act.dma_start(x_in[:, j, :], a["x"][i * 2 + j]).then_inc(x_setup_in, 16)
            act.wait_ge(stats_done, IMAGES)
            act.dma_start(x_in[:, 0, :], a["x"][0]).then_inc(x_next_in, 16)
            act.wait_ge(setup_pe, 6)
            act.activation(se[0:SPLITS, 10, :], ps[0:SPLITS, 5, 0:IMAGES], ACT.Exp, scale=-1.0).then_inc(setup_act, 1)
            act.wait_ge(setup_pe, 7)
            act.activation(se[:, 11, :], ps[:, 6, 0:IMAGES], ACT.Exp, scale=-1.0).then_inc(setup_act, 1)
            act.wait_ge(setup_pool, 3)

            def norm_out(k):
                act.wait_ge(back[0], k + 1)
                act.activation(norm_ch[:, :], flat(SIDE_A), ACT.Copy).then_inc(norm_done, 1)

            def high_part(k, lo, ready, parts, done):
                act.wait_ge(ready, k + 1)
                act.activation(parts[:, 0, :], flat(lo), ACT.Copy).then_inc(done, 1)

            def vz_out(k, r):
                for b in range(2 * r, 2 * r + 2):
                    act.wait_ge(vz_ready, k * 4 + b + 1)
                    pair = ps[:, SIDE_A + b % 2, :].rearrange("p (t w) -> p t w", t=2)
                    act.activation(v_aug[:, 2 * b:2 * b + 2, :, 0:DH],
                                   pair[:, :, 0:P].rearrange("p t (h d) -> p t h d", d=DH), ACT.Copy)
                    for t in range(2):
                        last = act.activation(z[:, 2 * b + t, :], pair[:, t, P:2 * P], ACT.Copy,
                                              scale=decay_norm[:, 2 * b + t:2 * b + t + 1])
                    last.then_inc(vz_done, 1)

            def n2_high_out(j):
                act.wait_ge(back[1], j + 1)
                act.activation(n2[:, 0, :], flat(SIDE_A), ACT.Copy).then_inc(n2_high, 1)

            def exp_gap(j):
                act.wait_ge(gap_done, j + 1)
                act.activation(gate_v[:, 3, :], gate_v[:, 2, :], ACT.Exp).then_inc(gap_exp, 1)

            def gates_out(j):
                act.wait_ge(gates_turned, j + 1)
                both = ps[0:3 * EXPERTS, SIDE_A:SIDE_A + 2, :].rearrange("p a b -> p (a b)")
                act.activation(gate_t[:, :], both, ACT.Copy).then_inc(gates_copied, 1)
                act.activation(gate_t_bf[:, :], both, ACT.Copy).then_inc(gates_copied, 1)

            def attention(i, j, ffn, prep):
                if prep:
                    act.wait_ge(turned[0], i + 2)
                    act.dma_start(x_in[:, 0, :], a["x"][i + 2]).then_inc(x_next_in, 16)
                if ffn:
                    act.wait_ge(t2_copied, i)
                else:
                    act.wait_ge(stats_done, IMAGES)
                act.dma_start(x_in[:, 1, :], a["x"][i]).then_inc(x_now_in, 16)
                for s in range(STEPS):
                    u, r = divmod(s, GROUP)
                    if ffn and s == AT_BACK2 + 2:
                        n2_high_out(j)
                    if ffn and s == AT_LOGITS + GAP_LAG:
                        exp_gap(j)
                    if ffn and s == AT_GATES + 2:
                        gates_out(j)
                    act.wait_ge(score_ready, i * STEPS + s + 1)
                    if u >= 2 and r == 0:
                        if u - 2 < TILES - 1:
                            act.wait_ge(value_done, i * VALUES_INC + u - 1)
                        elif u - 2 == TILES - 1:
                            act.wait_ge(half_done, i * 4 + 2)
                        else:
                            act.wait_ge(value_done, i * VALUES_INC + u - 2)
                    act.activation(probs[:, u % 2, r, :], flat(2 * (s % 2)), ACT.Exp,
                                   scale=DH ** -0.5).then_inc(exp_done, 1)

            def high_hidden(j, m):
                act.wait_ge(hidden_done, j * FFN_STEPS + m + 1)
                if m >= PART_BUFS:
                    act.wait_ge(hidden_used, j * FFN_STEPS + m - PART_BUFS + 1)
                act.activation(hid_high[m % PART_BUFS], hidden[m % HID_BUFS], ACT.Copy).then_inc(high_done, 1)

            def wide_out(j, w):
                act.wait_ge(wide_ready, j * WIDES + w + 1)
                if w >= WIDE_BUFS:
                    act.wait_ge(hidden_done, j * FFN_STEPS + FT * (w - WIDE_BUFS + 1))
                act.activation(gate_wide[w % WIDE_BUFS], ps[:, CB, :], ACT.Copy).then_inc(wide_done, 1)

            def store(j, c):
                act.wait_ge(result_done, j * HALVES + c + 1)
                act.dma_start(out[j, :, c * BANK:(c + 1) * BANK], t2[:, c * BANK:(c + 1) * BANK]).then_inc(stored, 16)

            def experts(i, j, ffn, nxt, prep):
                if ffn:
                    wide_out(j, 0)
                    wide_out(j, 1)
                    for m in range(AHEAD):
                        high_hidden(j, m)
                for m in range(FFN_STEPS):
                    if i is not None and m == AT_BACK_O:
                        act.wait_ge(on_back, i + 1)
                        act.activation(on_ch[:, :], flat(SIDE_B), ACT.Copy).then_inc(on_done, 1)
                    if nxt and m in AT_VZ:
                        vz_out(i + 1, AT_VZ.index(m))
                    if prep:
                        if m == AT_BACK1:
                            norm_out(i + 2)
                        if m == AT_Q:
                            act.wait_ge(rows_out, i * ROWS_INC + 2 * ROWS_INC)
                            high_part(i + 2, SIDE_A, q_ready, q_parts, q_high)
                        if m == AT_K:
                            high_part(i + 2, SIDE_B, k_ready, k_parts, k_high)
                    if ffn:
                        if m % 2 == 0 and m // 2 + 2 < WIDES:
                            wide_out(j, m // 2 + 2)
                        if m + AHEAD < FFN_STEPS:
                            high_hidden(j, m + AHEAD)
                        if m == SLICES + 1:
                            store(j, 0)
                if ffn:
                    store(j, 1)

            for k in range(2):
                norm_out(k)
                if k:
                    act.wait_ge(rows_out, ROWS_INC)
                high_part(k, SIDE_A, q_ready, q_parts, q_high)
                high_part(k, SIDE_B, k_ready, k_parts, k_high)
                if k == 0:
                    act.wait_ge(turned[0], 1)
                    act.dma_start(x_in[:, 0, :], a["x"][1]).then_inc(x_next_in, 16)
                    vz_out(0, 0)
                    vz_out(0, 1)
            attention(0, None, False, True)
            experts(0, None, False, True, True)
            with act.Fori(1, IMAGES - 2) as i:
                attention(i, i - 1, True, True)
                experts(i, i - 1, True, True, True)
            attention(IMAGES - 2, IMAGES - 3, True, False)
            experts(IMAGES - 2, IMAGES - 3, True, True, False)
            attention(IMAGES - 1, IMAGES - 2, True, False)
            experts(IMAGES - 1, IMAGES - 2, True, False, False)
            n2_high_out(IMAGES - 1)
            exp_gap(IMAGES - 1)
            gates_out(IMAGES - 1)
            experts(None, IMAGES - 1, True, False, False)
            act.wait_ge(stored, IMAGES * STORE_INC)

        @block.vector
        def _(dve):
            dve.wait_ge(const_in, CONST_INC)
            dve.tensor_copy(pick_bf[:, :], picks).then_inc(dot_done, 1)
            with dve.Fori(0, IMAGES // 2) as i:
                for j in range(2):
                    dve.wait_ge(x_setup_in, (i * 2 + j + 1) * 16)
                    dve.wait_ge(stats_done, i * 2 + j)
                    for c in range(HALVES):
                        last = dve.bn_stats(stat13[:, j, 6 * c:6 * c + 6], x_in[:, j, c * BANK:(c + 1) * BANK])
                    last.then_inc(bn_done, 1)
                    dve.wait_ge(dot_done, i * 2 + j + 1)
                    dve.tensor_tensor_reduce(dot_out, x_in[:, j, :], dct, 1.0, 0.0, ALU.mult, ALU.add,
                                             stat13[:, j, 12:13]).then_inc(dot_done, 1)
                    dve.wait_ge(bn_done, i * 2 + j + 1)
                    dve.wait_ge(dot_done, i * 2 + j + 2)
                    dve.tensor_copy(stats[:, i * 2 + j, :], stat13[:, j, :]).then_inc(stats_done, 1)
            dve.wait_ge(stats_done, IMAGES)
            for n in range(IMAGES):
                last = dve.bn_aggr(moments[:, n, :], stats[:, n, 0:12])
            last.then_inc(aggr_done, 1)
            dve.wait_ge(aggr_done, 1)

            links = [0]

            def link(ins):
                links[0] += 1
                ins.then_inc(setup_chain, 1)
                dve.wait_ge(setup_chain, links[0])

            link(dve.memset(k_stack[SHIFT_ROW:STACK, :, :], 1.0))
            dve.tensor_copy(se[:, 0, :], moments[:, :, 0]).then_inc(setup_dve, 1)
            dve.wait_ge(setup_pe, 1)
            link(dve.tensor_copy(offset[:, :], ps[:, 0, 0:IMAGES]))
            link(dve.tensor_tensor(se[:, 1, :], se[:, 0, :], offset[:, :], ALU.subtract))
            link(dve.tensor_tensor(se[:, 1, :], se[:, 1, :], se[:, 1, :], ALU.mult))
            dve.tensor_tensor(se[:, 2, :], se[:, 1, :], moments[:, :, 1], ALU.add).then_inc(setup_dve, 1)
            dve.wait_ge(setup_pe, 2)
            dve.tensor_scalar(se[:, 3, :], ps[:, 1, 0:IMAGES], 1e-5, None, ALU.add).then_inc(setup_dve, 1)
            dve.wait_ge(setup_dve, 3)
            link(dve.tensor_scalar(se[:, 1, :], offset[:, :], dct_sum[:, 0:1], None, ALU.mult))
            link(dve.tensor_tensor(se[:, 1, :], stats[:, :, 12], se[:, 1, :], ALU.subtract))
            dve.wait_ge(setup_pool, 4)
            dve.tensor_tensor(se[:, 5, :], se[:, 1, :], se[:, 4, :], ALU.mult).then_inc(setup_dve, 1)
            dve.wait_ge(setup_pe, 3)
            dve.tensor_copy(se[0:SPLITS, 6, :], ps[0:SPLITS, 2, 0:IMAGES]).then_inc(setup_dve, 1)
            dve.wait_ge(setup_pe, 5)
            dve.tensor_scalar(se[0:SPLITS, 7, :], ps[0:SPLITS, 3, 0:IMAGES], 0.0, None, ALU.max).then_inc(setup_dve, 1)
            dve.tensor_scalar(se[0:SPLITS * HID, 8, :], ps[0:SPLITS * HID, 4, 0:IMAGES], 0.0, None,
                              ALU.max).then_inc(setup_dve, 1)
            dve.wait_ge(setup_act, 1)
            link(dve.tensor_scalar(se[0:SPLITS, 10, :], se[0:SPLITS, 10, :], 1.0, None, ALU.add))
            dve.reciprocal(se[0:SPLITS, 9, :], se[0:SPLITS, 10, :]).then_inc(setup_dve, 1)
            dve.wait_ge(setup_act, 2)
            link(dve.tensor_scalar(se[:, 11, :], se[:, 11, :], 1.0, None, ALU.add))
            link(dve.reciprocal(se[:, 11, :], se[:, 11, :]))
            dve.wait_ge(setup_pe, 8)
            link(dve.tensor_tensor(se[:, 1, :], se[:, 11, :], ps[:, 7, 0:IMAGES], ALU.mult))
            link(dve.tensor_tensor(se[:, 2, :], se[:, 1, :], se[:, 4, :], ALU.mult))
            link(dve.tensor_scalar(slope[:, :], se[:, 2, :], 1.0, None, ALU.add))
            link(dve.scalar_tensor_tensor(offset[:, :], se[:, 2, :], -1.0, offset[:, :], ALU.mult, ALU.mult))
            dve.wait_ge(setup_pe, 9)
            dve.tensor_copy(wvz[:, P:2 * P], ps[:, 0, 0:P]).then_inc(setup_dve, 1)
            dve.wait_ge(setup_pe, 10)
            for r in range(3):
                last = dve.tensor_tensor(bias3[:, r, :], b2_t[:, :], ps[:, 1, 0:EXPERTS], ALU.add)
            last.then_inc(setup_dve, 1)
            link(dve.tensor_scalar(neg_b1[:, :], b1[:, :], -1.0, None, ALU.mult))
            dve.wait_ge(setup_pe, 11)
            link(dve.tensor_copy(bias_rows[:, :], ps[0:3 * EXPERTS, 2, 0:P]))
            dve.sem_inc(setup_done, 1)

            def affine(k):
                dve.wait_ge(x_next_in, (k + 1) * 16)
                dve.tensor_scalar(x_in[:, 0, :], x_in[:, 0, :], slope[:, bass.ds(k, 1)], offset[:, bass.ds(k, 1)],
                                  ALU.mult, ALU.add).then_inc(x1_done, 1)

            def residual(i):
                dve.wait_ge(x_now_in, (i + 1) * 16)
                dve.tensor_scalar(x_in[:, 1, :], x_in[:, 1, :], slope[:, bass.ds(i, 1)], offset[:, bass.ds(i, 1)],
                                  ALU.mult, ALU.add).then_inc(res_done, 1)

            def moments_of(k, j, lo):
                v = norm_v[:, j]
                base = k * NORM_CHAIN
                dve.wait_ge(turned[j], k + 1)
                for t in range(TILES):
                    last = dve.bn_stats(norm6[:, j, t, :], tiles(lo)[:, t, :])
                last.then_inc(bn_taken[j], 1)
                dve.wait_ge(bn_taken[j], k + 1)
                even, odd, s_even, s_odd = (norm6[:, j, :, c] for c in (1, 4, 2, 5))
                dve.tensor_tensor(v[:, 0, :], even, odd, ALU.add)
                dve.tensor_tensor(v[:, 1, :], even, odd, ALU.subtract)
                dve.tensor_tensor(v[:, 2, :], s_even, s_odd, ALU.add).then_inc(norm_step[j], 1)
                dve.wait_ge(norm_step[j], base + 1)
                dve.tensor_scalar(v[:, 3, :], v[:, 0, :], 0.5, None, ALU.mult)
                dve.tensor_tensor(v[:, 4, :], v[:, 1, :], v[:, 1, :], ALU.mult).then_inc(norm_step[j], 1)
                dve.wait_ge(norm_step[j], base + 2)
                dve.scalar_tensor_tensor(v[:, 5, :], v[:, 4, :], P / 4.0, v[:, 2, :], ALU.mult,
                                         ALU.add).then_inc(norm_step[j], 1)
                dve.wait_ge(norm_step[j], base + 3)
                dve.tensor_scalar(v[:, 6, :], v[:, 5, :], 1.0 / P, 1e-5, ALU.mult, ALU.add).then_inc(norm_step[j], 1)

            def normalise(k, j, lo):
                dve.wait_ge(rs_done[j], k + 1)
                for t in range(TILES):
                    last = dve.tensor_scalar(norm_tok[:, j, t, :], tiles(lo)[:, t, :], norm_v[:, j, 3, t:t + 1],
                                             norm_rs[:, j, t:t + 1], ALU.subtract, ALU.mult)
                last.then_inc(tok_done[j], 1)

            def split(k, n, lo, high, parts):
                base = (k * 2 + n) * SPLIT_CHAIN
                dve.wait_ge(high, k + 1)
                if not (n == 0 and isinstance(k, int) and k == 0):
                    dve.wait_ge(qk_split, k * 2 + n)
                dve.tensor_tensor(rest[:, :], flat(lo), parts[:, 0, :], ALU.subtract).then_inc(dve_split, 1)
                dve.wait_ge(dve_split, base + 1)
                dve.tensor_copy(parts[:, 1, :], rest[:, :]).then_inc(dve_split, 1)
                dve.wait_ge(dve_split, base + 2)
                dve.tensor_tensor(parts[:, 2, :], rest[:, :], parts[:, 1, :], ALU.subtract).then_inc(qk_split, 1)

            def maximum(k, n):
                for c in range(HALVES):
                    dve.wait_ge(full_ready, k * 2 * STEPS + 2 * n + c + 1)
                    dve.tensor_reduce(half_max[:, c, n:n + 1], ps[:, SIDE_A + c, :], AX.X, ALU.max).then_inc(max_done, 1)

            def shift(k, g):
                at = slice(g * GROUP_ROWS, (g + 1) * GROUP_ROWS)
                turn = k * 2 + g
                dve.wait_ge(max_done, k * 2 * STEPS + (g + 1) * STEPS)
                dve.tensor_tensor(row_max[:, at], half_max[:, 0, at], half_max[:, 1, at], ALU.max).then_inc(max_joined, 1)
                turned_max = ps[0:GROUP_ROWS, SIDE_A, 0:P]
                dve.wait_ge(max_turned, turn + 1)
                if not (isinstance(turn, int) and turn == 0):
                    dve.wait_ge(shift_in, turn * SHIFT_INC)
                dve.tensor_scalar(max_parts[:, 0, :], turned_max, -1.0, None, ALU.mult).then_inc(max_step, 1)
                dve.wait_ge(max_step, turn * MAX_CHAIN + 1)
                dve.scalar_tensor_tensor(max_rest[:, :], turned_max, -1.0, max_parts[:, 0, :], ALU.mult,
                                         ALU.subtract).then_inc(max_step, 1)
                dve.wait_ge(max_step, turn * MAX_CHAIN + 2)
                dve.tensor_copy(max_parts[:, 1, :], max_rest[:, :]).then_inc(max_step, 1)
                dve.wait_ge(max_step, turn * MAX_CHAIN + 3)
                dve.tensor_tensor(max_parts[:, 2, :], max_rest[:, :], max_parts[:, 1, :],
                                  ALU.subtract).then_inc(max_split, 1)

            def n2_low_out(j):
                dve.wait_ge(n2_high, j + 1)
                dve.tensor_tensor(n2[:, 1, :], flat(SIDE_A), n2[:, 0, :].bitcast(F32), ALU.subtract).then_inc(n2_done, 1)

            def choose(j):
                dve.wait_ge(logits_ready, j + 1)
                steps = [0]

                def then(ins, go=True):
                    steps[0] += 1
                    ins.then_inc(gate_step, 1)
                    if go:
                        dve.wait_ge(gate_step, j * GATE_CHAIN + steps[0])

                def by_expert(ap):
                    return ap.rearrange("p (t e) -> p t e", e=EXPERTS)

                def wide(ap):
                    return ap.unsqueeze(2).broadcast_to([P, TILES, EXPERTS])

                logits, is_best, score, rest_l = gate[:, 0, :], gate[:, 1, :], gate[:, 2, :], gate[:, 3, :]
                best, top, gap, weight = gate_v[:, 0, :], gate_v[:, 1, :], gate_v[:, 2, :], gate_v[:, 3, :]
                then(dve.tensor_tensor(logits, ps[:, SIDE_A, 0:TILES * EXPERTS], b_gate[:, :], ALU.add))
                then(dve.tensor_reduce(best, by_expert(logits), AX.X, ALU.max))
                for k in range(2):
                    src = logits if k == 0 else rest_l
                    value = best if k == 0 else gap
                    pick = gate[:, 4 + k, :]
                    then(dve.tensor_tensor(by_expert(is_best), by_expert(src), wide(value), ALU.is_equal))
                    then(dve.tensor_tensor(score, is_best, rank[:, :], ALU.mult))
                    then(dve.tensor_reduce(top, by_expert(score), AX.X, ALU.max))
                    then(dve.tensor_tensor(by_expert(pick), by_expert(rank[:, :]), wide(top), ALU.is_equal))
                    if k == 0:
                        then(dve.scalar_tensor_tensor(rest_l, pick, -3.0e38, logits, ALU.mult, ALU.add))
                        then(dve.tensor_reduce(gap, by_expert(rest_l), AX.X, ALU.max))
                dve.tensor_tensor(gate_v[:, 2, :], gap, best, ALU.subtract).then_inc(gap_done, 1)
                dve.wait_ge(gap_exp, j + 1)
                then(dve.tensor_scalar(gate_v[:, 4, :], weight, 1.0, None, ALU.add))
                then(dve.reciprocal(gate_v[:, 5, :], gate_v[:, 4, :]))
                then(dve.tensor_tensor(gate_v[:, 6, :], weight, gate_v[:, 5, :], ALU.mult))
                then(dve.tensor_tensor(by_expert(gate[:, 6, :]), by_expert(gate[:, 4, :]), wide(gate_v[:, 5, :]), ALU.mult),
                     go=False)
                then(dve.tensor_tensor(by_expert(gate[:, 7, :]), by_expert(gate[:, 5, :]), wide(gate_v[:, 6, :]), ALU.mult))
                then(dve.tensor_tensor(gate[:, 0, :], gate[:, 6, :], gate[:, 7, :], ALU.add))
                for r in range(2):
                    then(dve.tensor_copy(gate_bf[:, :], gate[:, r, :]))
                    then(dve.tensor_copy(gate3[:, :, r, :], by_expert(gate_bf[:, :])), go=False)
                    then(dve.tensor_tensor(gate[:, r + 1, :], gate[:, r, :], gate_bf[:, :], ALU.subtract))
                dve.tensor_copy(gate3[:, :, 2, :], by_expert(gate[:, 2, :])).then_inc(gates_done, 1)
                assert steps[0] == GATE_CHAIN, steps[0]

            def copy_o(i, g, c):
                dve.wait_ge(half_done, i * 4 + 2 * g + c + 1)
                dve.tensor_copy(o_sb[g][:, c * BANK:(c + 1) * BANK], ps[:, O_BANKS + c, :]).then_inc(o_copied, 1)

            def attention(i, j, ffn, nxt):
                for s in range(STEPS):
                    if s == AT_COPY_O[0]:
                        copy_o(i, 0, 0)
                    if s == AT_COPY_O[1]:
                        copy_o(i, 0, 1)
                    if s < len(MAX_SECOND):
                        maximum(i, MAX_SECOND[s])
                    if s == AT_SHIFT2:
                        shift(i, 1)
                    if ffn and s == AT_BACK2:
                        n2_low_out(j)
                    if ffn and s == AT_LOGITS:
                        choose(j)
                    if nxt and AT_FIRST <= s < AT_FIRST + IN_SCORES:
                        maximum(i + 1, s - AT_FIRST)
                dve.wait_ge(rows_out, i * ROWS_INC + 2 * ROWS_INC if nxt else i * ROWS_INC + ROWS_INC)
                copy_o(i, 1, 0)
                copy_o(i, 1, 1)

            def scale_o(i, g):
                by_head = tiles(SIDE_B).rearrange("p t (r w) -> p t r w", w=32)
                dve.wait_ge(o_turned, i * 2 + g + 1)
                dve.reciprocal(o_recip[:, g, :, :], by_head[:, :, :, DH]).then_inc(recip_done, 1)
                dve.wait_ge(recip_done, i * 2 + g + 1)
                dve.tensor_tensor(on_tok.rearrange("p t (h d) -> p t h d", d=DH)[:, :, g * GROUP:(g + 1) * GROUP, :],
                                  by_head[:, :, :, 0:DH],
                                  o_recip[:, g, :, :].unsqueeze(3).broadcast_to([P, TILES, GROUP, DH]),
                                  ALU.mult).then_inc(o_scaled, 1)

            def add_attention(i):
                dve.wait_ge(attn_ready, i + 1)
                dve.wait_ge(res_done, i + 1)
                dve.scalar_tensor_tensor(t2_next, flat(SIDE_B), b_out[:, 0:1], x_in[:, 1, :], ALU.add,
                                         ALU.add).then_inc(t2_done, 1)

            def activate(j, m):
                n, w = m % SLICES, m // FT
                dve.wait_ge(hidden_ready, j * FFN_STEPS + m + 1)
                dve.wait_ge(wide_done, j * WIDES + w + 1)
                if m >= HID_BUFS:
                    dve.wait_ge(low_done, j * FFN_STEPS + m - HID_BUFS + 1)
                dve.scalar_tensor_tensor(hidden[m % HID_BUFS], ps[:, m % 2, :], neg_b1[:, n:n + 1],
                                         gate_wide[w % WIDE_BUFS], ALU.max, ALU.mult).then_inc(hidden_done, 1)

            def result(j, c):
                at = slice(c * BANK, (c + 1) * BANK)
                dve.wait_ge(hidden_used, j * FFN_STEPS + (c + 1) * SLICES)
                dve.wait_ge(t2_copied, j + 1)
                dve.tensor_tensor(t2[:, at], t2[:, at], ps[:, YB, :], ALU.add).then_inc(result_done, 1)

            def experts(i, j, ffn, nxt, prep):
                if ffn:
                    for m in range(AHEAD):
                        activate(j, m)
                for m in range(FFN_STEPS):
                    if ffn and m == SLICES:
                        result(j, 0)
                    if nxt and m in MAX_TAIL:
                        maximum(i + 1, MAX_TAIL[m])
                    if nxt and m == AT_SHIFT1:
                        shift(i + 1, 0)
                    if nxt and m in MAX_EARLY:
                        for n in MAX_EARLY[m]:
                            maximum(i + 1, n)
                    if i is not None:
                        if m in AT_TURN_O:
                            scale_o(i, AT_TURN_O.index(m))
                        if m == AT_RESIDUAL:
                            residual(i)
                        if m == AT_OUT:
                            add_attention(i)
                        if m == AT_TURN_T2 + 1:
                            moments_of(i, 1, SIDE_B)
                        if m == AT_NORM2:
                            normalise(i, 1, SIDE_B)
                    if prep:
                        if m == AT_AFFINE:
                            affine(i + 2)
                        if m == AT_TURN_X + 1:
                            moments_of(i + 2, 0, SIDE_A)
                        if m == AT_NORM1:
                            normalise(i + 2, 0, SIDE_A)
                        if m == AT_Q:
                            split(i + 2, 0, SIDE_A, q_high, q_parts)
                        if m == AT_K:
                            split(i + 2, 1, SIDE_B, k_high, k_parts)
                    if ffn and m + AHEAD < FFN_STEPS:
                        activate(j, m + AHEAD)
                if ffn:
                    result(j, 1)

            for k in range(2):
                affine(k)
                moments_of(k, 0, SIDE_A)
                normalise(k, 0, SIDE_A)
                split(k, 0, SIDE_A, q_high, q_parts)
                split(k, 1, SIDE_B, k_high, k_parts)
            for w, raw in ((w_in, w_in_raw), (w_out, w_out_raw)):
                view = raw.rearrange("p (n c) -> p n c", c=P)
                link(dve.tensor_copy(w[:, 0, :, :], view))
                link(dve.tensor_tensor(w[:, 1, :, :], view, w[:, 0, :, :].bitcast(F32), ALU.subtract))
            dve.sem_inc(setup_done, 1)
            for n in range(GROUP_ROWS):
                maximum(0, n)
            shift(0, 0)
            for n in range(GROUP_ROWS, MAX_SECOND[0]):
                maximum(0, n)

            attention(0, None, False, True)
            experts(0, None, False, True, True)
            with dve.Fori(1, IMAGES - 2) as i:
                attention(i, i - 1, True, True)
                experts(i, i - 1, True, True, True)
            attention(IMAGES - 2, IMAGES - 3, True, True)
            experts(IMAGES - 2, IMAGES - 3, True, True, False)
            attention(IMAGES - 1, IMAGES - 2, True, False)
            experts(IMAGES - 1, IMAGES - 2, True, False, False)
            n2_low_out(IMAGES - 1)
            choose(IMAGES - 1)
            experts(None, IMAGES - 1, True, False, False)


_NAMES = ["L0_conv_W1", "L0_conv_W2", "L0_conv_M1", "L0_conv_M2", "L1_attn_W_qkv", "L1_attn_W_out",
          "L1_attn_b_out", "L1_ffn_w1", "L1_ffn_b1", "L1_ffn_w2", "L1_ffn_b2", "L1_ffn_wg", "L1_ffn_bg"]


def laid_out(x, w):
    c = np.ascontiguousarray
    qkvt, out = w["L1_attn_W_qkv"], w["L1_attn_W_out"].reshape(HEADS, 2, DH, P)
    w1_blocks = np.zeros((P, SPLITS * HID), np.float32)
    w2_blocks = np.zeros((SPLITS * HID, P), np.float32)
    for g in range(SPLITS):
        w1_blocks[g * CP_SPLIT:(g + 1) * CP_SPLIT, g * HID:(g + 1) * HID] = w["L0_conv_W1"][g].T
        w2_blocks[g * HID:(g + 1) * HID, g * CP_SPLIT:(g + 1) * CP_SPLIT] = w["L0_conv_W2"][g].T

    def by_dim(m):
        return c(m.reshape(P, HEADS, DH).transpose(0, 2, 1).reshape(P, P))

    return {
        "x": c(x.reshape(IMAGES, P, TOK)),
        "m1_t": c(w["L0_conv_M1"].T), "m2_t": c(w["L0_conv_M2"].T),
        "w1_blocks": w1_blocks, "w2_blocks": w2_blocks, "wo1": c(out[:, 0].reshape(P, P)),
        "wq": by_dim(qkvt[:, 0:P]), "wk": by_dim(qkvt[:, P:2 * P]), "wv": c(qkvt[:, 2 * P:3 * P]),
        "wt_t": c(qkvt[:, 3 * P:4 * P].T), "wo2": c(out[:, 1].reshape(P, P)),
        "b_out": c(w["L1_attn_b_out"].reshape(P, 1)),
        "w_in": c(w["L1_ffn_w1"].reshape(EXPERTS, P, FT, P).transpose(1, 0, 2, 3).reshape(P, SLICES * P)),
        "w_out": c(w["L1_ffn_w2"].reshape(EXPERTS, FT, P, P).transpose(2, 0, 1, 3).reshape(P, SLICES * P)),
        "b1": c(w["L1_ffn_b1"].reshape(SLICES, P).T), "b2_t": c(w["L1_ffn_b2"].T),
        "w_gate": c(w["L1_ffn_wg"]), "b_gate": c(np.broadcast_to(w["L1_ffn_bg"], (TILES, EXPERTS))),
    }


def kernel(**inputs):
    import concourse.bacc as bacc
    from concourse.bass_utils import run_bass_kernel_spmd

    x = np.asarray(inputs["x"])
    arrays = laid_out(x, {n: np.asarray(inputs[n]) for n in _NAMES})
    arrays.update(shape_constants())
    nc = bacc.Bacc("TRN2", target_bir_lowering=False, num_devices=1)
    a = {n: nc.dram_tensor(f"in_{n}", v.shape, F32, kind="ExternalInput").ap() for n, v in arrays.items()}
    out = nc.dram_tensor("out", (IMAGES, P, TOK), F32, kind="ExternalOutput").ap()
    build(nc, a, out)
    r = run_bass_kernel_spmd(nc, [{f"in_{n}": v for n, v in arrays.items()}], core_ids=[0])
    return r.results[0]["out"].reshape(x.shape)
```

```python
from contextlib import ExitStack

import numpy as np

import concourse.bass as bass
from concourse import mybir

F32 = mybir.dt.float32
BF16 = mybir.dt.bfloat16
F32R = mybir.dt.float32r
ALU = mybir.AluOpType
ACT = mybir.ActivationFunctionType
AX = mybir.AxisListType

P = 128
IMAGES = 16
SIDE = 32
TOK = SIDE * SIDE
TILES = TOK // P
BANK = 512
HALVES = TOK // BANK
HEADS, DH = 8, 16
GROUP = 4
GROUPS = HEADS // GROUP
SPLITS = 8
CP_SPLIT = P // SPLITS
HID = P // 16
NORM_GROUP = 4
EXPERTS, FF = 8, 256
FT = FF // P
SLICES = EXPERTS * FT
REACH = 2
STRIP = (2 * REACH + 1) * P
PAIRS = 6
SHIFT_ROW = PAIRS * DH
STACK = SHIFT_ROW + 3
X_BUFS = 4
STEPS = HEADS * TILES
QUADS = GROUPS * TILES
GROUP_ROWS = GROUP * TILES
FFN_STEPS = HALVES * SLICES
GATE_ROWS = 3 * 3 * EXPERTS
WIDES = HALVES * EXPERTS
AHEAD = 3
HID_BUFS, PART_BUFS, WIDE_BUFS = 5, 3, 3
ROWS_INC = PAIRS * 16
STACK_INC = 2 * 16
SHIFT_INC = 3 * 16
STORE_INC = HALVES * 16
VALUES_INC = QUADS - GROUPS
NORM_CHAIN, ROOT_CHAIN, SPLIT_CHAIN, MAX_CHAIN, GATE_CHAIN = 4, 2, 2, 3, 25
SECOND_STEPS = (0, 1, 2, 3, 5, 6, 7, 8, 10, 11, 12, 13, 15, 16, 17, 18, 21, 22, 23)
FIRST_STEPS = (37, 39, 40, 41, 42, 43, 45, 46, 47, 48, 50, 51, 52, 54, 55, 56, 57, 58, 60, 61, 62, 63)
FIRST_SLICES = (0, 1, 2, 3, 4, 5, 6, 7, 8, 9)
SECOND_SLICES = (11, 12, 18, 19, 20, 21, 22, 23, 25, 26, 28, 30)
MAX_TAIL = len(FIRST_STEPS)
MAX_EARLY = STEPS - len(SECOND_STEPS)
MAX_ON_B = range(34, 39)
MAX_AFTER_PREP = MAX_ON_B[-1] + 1
MAX_SECOND = dict(zip(SECOND_STEPS, range(MAX_EARLY, STEPS)))
MAX_FIRST = dict(zip(FIRST_STEPS, range(MAX_TAIL)))
MAX_BESIDE = dict(zip(FIRST_SLICES, range(MAX_TAIL, GROUP_ROWS)))
MAX_BESIDE.update(zip(SECOND_SLICES, range(GROUP_ROWS, MAX_EARLY - 1)))
AT_SHIFT1 = max(FIRST_SLICES) + 1
QK_BESIDE = (4, 8)
AT_FIRST = min(MAX_FIRST)
AT_SHIFT2 = max(SECOND_STEPS) + 1
AT_BACK2, AT_LOGITS, AT_GATES = 27, 29, 36
GAP_LAG = 4
AT_COPY_O = (33, 35)
VALUES_AT = (0, 2)
AT_LOAD = 12
AT_TURN_O, AT_BACK_O = (1, 4), 5
DECAY_TILES = {6: (0, 1), 7: (2, 3), 8: (4, 5), 9: (6, 7)}
AT_OUT, AT_RESIDUAL, AT_TURN_T2, AT_ROOT2, AT_NORM2 = 10, 4, 11, 12, 15
AT_VZ = (19, 20)
AT_AFFINE, AT_TURN_X, AT_ROOT1, AT_NORM1, AT_BACK1, AT_Q, AT_K = 5, 13, 14, 17, 21, 23, 25
AT_NEXT = 30
DCT_X = (0, 0, 1, -1, 0, 3, 0, 2)
DCT_Y = (0, 1, 0, -1, 3, 0, 2, 0)


def shape_constants():
    def basis(freq):
        r = np.cos(np.pi * freq * (np.arange(SIDE) + 0.5) / SIDE) / np.sqrt(SIDE)
        return r * np.sqrt(2.0) if freq != 0 else r

    c = {}
    dct = np.zeros((P, SIDE, SIDE), np.float32)
    for i, (u, v) in enumerate(zip(DCT_X, DCT_Y)):
        dct[i * CP_SPLIT:(i + 1) * CP_SPLIT] = np.outer(basis(u), basis(v)).astype(np.float32)
    c["dct"] = dct.reshape(P, TOK)
    c["dct_sum"] = dct.astype(np.float64).sum((1, 2)).astype(np.float32).reshape(P, 1)
    ch = np.arange(P)
    c["ident"] = np.eye(P, dtype=np.float32)
    c["group_mean"] = (ch[:, None] // NORM_GROUP == ch[None] // NORM_GROUP).astype(np.float32) / NORM_GROUP
    member = (ch[:, None] // CP_SPLIT == np.arange(SPLITS)[None]).astype(np.float32)
    c["split_mean"] = member / CP_SPLIT
    c["split_spread"] = np.ascontiguousarray(member.T)
    dist = np.abs(np.arange(STRIP)[None] - REACH * P - ch[:, None]).astype(np.float32)
    c["decay"] = np.exp(-dist / np.float32(np.e)).astype(np.float32)
    pos = np.arange(TOK, dtype=np.float32)
    full = np.exp(-np.abs(pos[None] - pos[:, None]) / np.float32(np.e)).astype(np.float32)
    c["decay_norm"] = np.ascontiguousarray((1.0 / full.sum(-1)).astype(np.float32).reshape(TILES, P).T)
    pick = np.zeros((3, EXPERTS, EXPERTS, P), np.float32)
    for e in range(EXPERTS):
        pick[:, e, e] = 1.0
    c["gate_pick"] = pick.reshape(3 * EXPERTS, EXPERTS * P)
    c["rank"] = np.tile((EXPERTS - np.arange(EXPERTS)).astype(np.float32), (P, TILES))
    return {k: np.ascontiguousarray(v, dtype=np.float32) for k, v in c.items()}


def build(nc, a, out):
    nc.disable_value_cache = True
    with ExitStack() as ctx:
        def sb(name, shape, dt=F32):
            return ctx.enter_context(nc.sbuf_tensor(name, shape, dt))

        def sem(name):
            return ctx.enter_context(nc.semaphore(name))

        dct_sum = sb("dct_sum", [P, 1])
        ident = sb("ident", [P, P])
        split_mean = sb("split_mean", [P, SPLITS])
        split_spread = sb("split_spread", [SPLITS, P])
        decay = sb("decay", [P, STRIP])
        decay_norm = sb("decay_norm", [P, TILES])
        rank = sb("rank", [P, TILES * EXPERTS])
        pick_bf = sb("pick_bf", [3 * EXPERTS, EXPERTS * P], BF16)
        m1_t = sb("m1_t", [SPLITS, SPLITS])
        m2_t = sb("m2_t", [SPLITS, SPLITS])
        wq = sb("wq", [P, P])
        wk = sb("wk", [P, P])
        wvz = sb("wvz", [P, 2 * P])
        wo1 = sb("wo1", [P, P])
        b_out = sb("b_out", [P, 1])
        w_in = sb("w_in", [P, 2, SLICES, P], F32R)
        w_out = sb("w_out", [P, 2, SLICES, P], F32R)
        b1 = sb("b1", [P, SLICES])
        neg_b1 = sb("neg_b1", [P, SLICES])
        b2_t = sb("b2_t", [P, EXPERTS])
        w_gate = sb("w_gate", [P, EXPERTS])
        b_gate = sb("b_gate", [P, TILES * EXPERTS])
        bias9 = sb("bias9", [P, 3, 3, EXPERTS])
        bias_bf = sb("bias_bf", [P, EXPERTS], BF16)
        bias_rest = sb("bias_rest", [P, 3, EXPERTS])
        bias_rows = sb("bias_rows", [GATE_ROWS, P], BF16)
        minus_half = sb("minus_half", [P, IMAGES])
        zero = sb("zero", [P, 1])

        stat13 = sb("stat13", [P, 2, 13])
        moments = sb("moments", [P, IMAGES, 2])
        stats = sb("stats", [P, IMAGES, 13])
        se = sb("se", [P, 12, IMAGES])
        slope = sb("slope", [P, IMAGES])
        offset = sb("offset", [P, IMAGES])

        x_in = sb("x_in", [P, 2, TOK])
        norm6 = sb("norm6", [P, 2, TILES, 6])
        norm_v = sb("norm_v", [P, 2, 7, TILES])
        norm_rs = sb("norm_rs", [P, 2, 3, TILES])
        norm_tok = sb("norm_tok", [P, 2, TILES, P])
        x_buf = [x_in[:, n, :] for n in range(2)] \
            + [norm_tok[:, n, :, :].rearrange("p t c -> p (t c)") for n in range(2)]
        on_tok = norm_tok[:, 0, :, :]
        norm_ch = sb("norm_ch", [P, TOK])
        q_parts = sb("q_parts", [P, 3, TOK], BF16)
        k_parts = sb("k_parts", [P, 3, TOK], BF16)
        rest = sb("rest", [P, TOK])
        on_ch = rest
        q_rest = x_in[:, 0, :]
        q_stack = sb("q_stack", [STACK, HEADS, TOK], BF16)
        k_stack = sb("k_stack", [STACK, HEADS, TOK], BF16)
        v_aug = sb("v_aug", [P, TILES, HEADS, 32])
        z = sb("z", [P, TILES, P])
        half_max = sb("half_max", [P, HALVES, STEPS])
        row_max = sb("row_max", [P, STEPS])
        max_parts = sb("max_parts", [GROUP_ROWS, 3, P], BF16)
        max_rest = sb("max_rest", [GROUP_ROWS, P])
        o_sb = (rest[:, :], k_parts[:, 0:2, :].rearrange("p a b -> p (a b)").bitcast(F32))
        o_recip = sb("o_recip", [P, GROUPS, TILES, GROUP])
        t2 = sb("t2", [P, TOK])
        t2_next = x_in[:, 1, :]
        n2 = sb("n2", [P, 2, TOK], F32R)
        gate = sb("gate", [P, 8, TILES * EXPERTS])
        gate_v = sb("gate_v", [P, 8, TILES])
        gate_bf = sb("gate_bf", [P, TILES * EXPERTS], BF16)
        gate9 = sb("gate9", [P, TILES, 3, 3, EXPERTS])
        gate_t = sb("gate_t", [GATE_ROWS, TOK], BF16)

        region = sb("region", [P, 2 * GROUP * TOK])
        taken = [0]

        def part(cols, rows=P):
            taken[0] += cols
            assert taken[0] <= 2 * GROUP * TOK
            return region[0:rows, taken[0] - cols:taken[0]]

        w_in_raw, w_out_raw = part(SLICES * P), part(SLICES * P)
        dct, dot_out, picks = part(TOK), part(TOK), part(TOK, 3 * EXPERTS)
        group_mean, wt_t, wo2 = part(P), part(P), part(P)
        w1_blocks, w2_blocks = part(SPLITS * HID), part(P, SPLITS * HID)
        probs = region[:, :].rearrange("p (u i t) -> p u i t", u=2, i=GROUP)
        taken[0] = GROUP * TOK
        hidden = [part(BANK) for _ in range(HID_BUFS)]
        gate_wide = [part(BANK) for _ in range(WIDE_BUFS)]

        hid_parts = sb("hid_parts", [P, 2, PART_BUFS, BANK], F32R)
        hid_high = [hid_parts[:, 0, k, :] for k in range(PART_BUFS)]
        hid_low = [hid_parts[:, 1, k, :] for k in range(PART_BUFS)]

        ps = ctx.enter_context(nc.psum_tensor("ps", [P, 8, BANK], F32))
        SIDE_A, SIDE_B, O_BANKS = 4, 6, 6
        CB, YB = 2, 3

        q_rows = nc.dram_tensor("q_rows", (PAIRS, P, TOK), BF16, kind="Internal").ap()
        k_rows = nc.dram_tensor("k_rows", (PAIRS, P, TOK), BF16, kind="Internal").ap()

        const_in = sem("const_in")
        dct_in = sem("dct_in")
        x_setup_in = [sem(f"x_setup_in{n}") for n in range(X_BUFS)]
        stats_done = sem("stats_done")
        setup_pe = sem("setup_pe")
        setup_dve = sem("setup_dve")
        setup_act = sem("setup_act")
        setup_pool = sem("setup_pool")
        setup_chain = sem("setup_chain")
        setup_done = sem("setup_done")
        bn_done = sem("bn_done")
        dot_done = sem("dot_done")
        aggr_done = sem("aggr_done")
        x_next_in = sem("x_next_in")
        x_now_in = sem("x_now_in")
        x1_done = sem("x1_done")
        res_done = sem("res_done")
        turned = [sem(f"turned{k}") for k in (1, 2)]
        bn_taken = [sem(f"bn_taken{k}") for k in (1, 2)]
        norm_step = [sem(f"norm_step{k}") for k in (1, 2)]
        root_step = [sem(f"root_step{k}") for k in (1, 2)]
        rs_done = [sem(f"rs_done{k}") for k in (1, 2)]
        tok_done = [sem(f"tok_done{k}") for k in (1, 2)]
        back = [sem(f"back{k}") for k in (1, 2)]
        norm_done = sem("norm_done")
        n2_high = sem("n2_high")
        n2_done = sem("n2_done")
        q_ready = sem("q_ready")
        k_ready = sem("k_ready")
        q_high = sem("q_high")
        k_high = sem("k_high")
        qk_split = sem("qk_split")
        dve_split = sem("dve_split")
        rows_out = sem("rows_out")
        stack_in = [sem(f"stack_in{p}") for p in range(HEADS // 2)]
        vz_ready = sem("vz_ready")
        vz_done = sem("vz_done")
        full_ready = sem("full_ready")
        max_done = sem("max_done")
        max_joined = sem("max_joined")
        max_turned = sem("max_turned")
        max_step = sem("max_step")
        max_split = sem("max_split")
        shift_in = sem("shift_in")
        score_ready = sem("score_ready")
        exp_done = sem("exp_done")
        value_done = sem("value_done")
        half_done = sem("half_done")
        o_copied = sem("o_copied")
        o_turned = sem("o_turned")
        recip_done = sem("recip_done")
        o_scaled = sem("o_scaled")
        on_back = sem("on_back")
        on_done = sem("on_done")
        attn_ready = sem("attn_ready")
        t2_done = sem("t2_done")
        t2_copied = sem("t2_copied")
        logits_ready = sem("logits_ready")
        gate_step = sem("gate_step")
        gap_done = sem("gap_done")
        gap_exp = sem("gap_exp")
        gates_done = sem("gates_done")
        gates_turned = sem("gates_turned")
        gates_copied = sem("gates_copied")
        wide_ready = sem("wide_ready")
        wide_done = sem("wide_done")
        hidden_ready = sem("hidden_ready")
        hidden_done = sem("hidden_done")
        high_done = sem("high_done")
        low_done = sem("low_done")
        hidden_used = sem("hidden_used")
        result_done = sem("result_done")
        stored = sem("stored")

        consts = [(dct_sum[:, :], "dct_sum"), (ident[:, :], "ident"), (group_mean, "group_mean"),
                  (split_mean[:, :], "split_mean"), (split_spread[:, :], "split_spread"),
                  (decay[:, :], "decay"), (decay_norm[:, :], "decay_norm"), (rank[:, :], "rank"),
                  (m1_t[:, :], "m1_t"), (m2_t[:, :], "m2_t"), (w1_blocks, "w1_blocks"), (w2_blocks, "w2_blocks"),
                  (wq[:, :], "wq"), (wk[:, :], "wk"), (wvz[:, 0:P], "wv"), (wo1[:, :], "wo1"), (wt_t, "wt_t"),
                  (wo2, "wo2"), (b_out[:, :], "b_out"), (b1[:, :], "b1"), (b2_t[:, :], "b2_t"),
                  (w_gate[:, :], "w_gate"), (picks, "gate_pick"), (w_in_raw, "w_in"), (w_out_raw, "w_out"),
                  (b_gate[:, :].rearrange("p (t e) -> p t e", t=TILES), "b_gate")]
        CONST_INC = 16 * len(consts)

        def flat(lo):
            return ps[:, lo:lo + 2, :].rearrange("p a b -> p (a b)")

        def max_bank(n):
            return SIDE_B if n in MAX_ON_B else SIDE_A

        def tiles(lo):
            return ps[:, lo:lo + 2, :].rearrange("p a (b c) -> p (a b) c", c=P)

        block = ctx.enter_context(nc.Block())

        @block.sync
        def _(sp):
            sp.dma_start(dct, a["dct"]).then_inc(dct_in, 16)
            for tile, name in consts:
                src = a[name]
                if name == "b_gate":
                    src = src.unsqueeze(0).broadcast_to([P, TILES, EXPERTS])
                sp.dma_start(tile, src).then_inc(const_in, 16)

            def rows_to_dram(q_split, k_split, spent):
                sp.wait_ge(qk_split, q_split)
                if spent is not None:
                    for p in range(HEADS // 2):
                        sp.wait_ge(stack_in[p], spent)
                sp.dma_start(q_rows[0:3].rearrange("s p t -> p s t"),
                             q_parts[:, 0:1, :].broadcast_to([P, 3, TOK])).then_inc(rows_out, 16)
                sp.dma_start(q_rows[3:5].rearrange("s p t -> p s t"),
                             q_parts[:, 1:2, :].broadcast_to([P, 2, TOK])).then_inc(rows_out, 16)
                sp.dma_start(q_rows[5], q_parts[:, 2, :]).then_inc(rows_out, 16)
                sp.wait_ge(qk_split, k_split)
                sp.dma_start(k_rows[0:3].rearrange("s p t -> p s t"), k_parts[:, 0:3, :]).then_inc(rows_out, 16)
                sp.dma_start(k_rows[3:5].rearrange("s p t -> p s t"), k_parts[:, 0:2, :]).then_inc(rows_out, 16)
                sp.dma_start(k_rows[5], k_parts[:, 0, :]).then_inc(rows_out, 16)

            def load_stacks(g):
                for p in range(2):
                    heads = slice(g * GROUP + 2 * p, g * GROUP + 2 * p + 2)
                    for stack, rows in ((q_stack, q_rows), (k_stack, k_rows)):
                        by_row = rows.rearrange("s (d h) t -> (s d) h t", h=HEADS)
                        sp.dma_start(stack[0:SHIFT_ROW, heads, :],
                                     by_row[:, heads, :]).then_inc(stack_in[2 * g + p], 16)

            def load_shift(g):
                for j in range(3):
                    sp.dma_start(q_stack[SHIFT_ROW + j:SHIFT_ROW + j + 1, g * GROUP:(g + 1) * GROUP, :]
                                 .rearrange("p h (t q) -> p (h t) q", q=P),
                                 max_parts[:, j, :]).then_inc(shift_in, 16)

            rows_to_dram(1, 2, None)
            sp.wait_ge(rows_out, ROWS_INC)
            load_stacks(0)
            load_stacks(1)
            rows_to_dram(3, 4, STACK_INC)
            sp.wait_ge(max_split, 1)
            load_shift(0)

            def image(i, nxt, prep):
                def count(each, more):
                    return i * each + more if isinstance(i, int) else sp.snap(i * each + more)

                second_max, first_max = count(2, 2), count(2, 3)
                middle, after = count(STEPS, STEPS // 2), count(STEPS, STEPS)
                written, loaded = count(ROWS_INC, 2 * ROWS_INC), count(STACK_INC, 2 * STACK_INC)
                q_split, k_split = count(2, 5), count(2, 6)
                sp.wait_ge(max_split, second_max)
                load_shift(1)
                if nxt:
                    sp.wait_ge(rows_out, written)
                    sp.wait_ge(score_ready, middle)
                    load_stacks(0)
                    sp.wait_ge(score_ready, after)
                    load_stacks(1)
                    sp.wait_ge(max_split, first_max)
                    load_shift(0)
                if prep:
                    rows_to_dram(q_split, k_split, loaded)

            image(0, True, True)
            with sp.Fori(1, IMAGES - 2) as i:
                image(i, True, True)
            image(IMAGES - 2, True, False)
            image(IMAGES - 1, False, False)
            sp.wait_ge(rows_out, IMAGES * ROWS_INC)

        @block.gpsimd
        def _(pool):
            pool.memset(minus_half[:, :], -0.5).then_inc(setup_pool, 1)
            pool.memset(v_aug[:, :, :, :], 0.0).then_inc(setup_pool, 1)
            pool.wait_ge(setup_pool, 2)
            pool.memset(v_aug[:, :, :, DH:DH + 1], 1.0).then_inc(setup_pool, 1)
            pool.memset(zero[:, :], 0.0).then_inc(setup_pool, 1)
            pool.wait_ge(setup_pool, 4)
            pool.wait_ge(setup_dve, 3)
            pool.tensor_tensor(se[:, 4, :], se[:, 3, :], minus_half[:, :], ALU.pow).then_inc(setup_pool, 1)

            def reciprocal_root(k, j):
                pool.wait_ge(norm_step[j], (k + 1) * NORM_CHAIN)
                pool.tensor_tensor(norm_rs[:, j, 0, :], norm_v[:, j, 6, :], minus_half[:, 0:TILES],
                                   ALU.pow).then_inc(root_step[j], 1)
                pool.wait_ge(root_step[j], k * ROOT_CHAIN + 1)
                pool.tensor_tensor(norm_rs[:, j, 1, :], norm_v[:, j, 3, :], norm_rs[:, j, 0, :],
                                   ALU.mult).then_inc(root_step[j], 1)
                pool.wait_ge(root_step[j], k * ROOT_CHAIN + 2)
                pool.tensor_tensor(norm_rs[:, j, 2, :], zero[:, :].broadcast_to([P, TILES]), norm_rs[:, j, 1, :],
                                   ALU.subtract).then_inc(rs_done[j], 1)

            def split(k, n, parts, scratch):
                pool.wait_ge(dve_split, (k * 2 + n + 1) * SPLIT_CHAIN)
                pool.tensor_tensor(parts[:, 2, :], scratch, parts[:, 1, :], ALU.subtract).then_inc(qk_split, 1)

            def low_part(j, m):
                pool.wait_ge(high_done, j * FFN_STEPS + m + 1)
                pool.tensor_tensor(hid_low[m % PART_BUFS], hidden[m % HID_BUFS],
                                   hid_high[m % PART_BUFS].bitcast(F32), ALU.subtract).then_inc(low_done, 1)

            def experts(i, j, ffn, nxt, prep):
                if ffn:
                    for m in range(AHEAD):
                        low_part(j, m)
                for m in range(FFN_STEPS):
                    if i is not None and m == AT_ROOT2:
                        reciprocal_root(i, 1)
                    if prep and m == AT_ROOT1:
                        reciprocal_root(i + 2, 0)
                    if prep and m == AT_Q:
                        split(i + 2, 0, q_parts, q_rest)
                    if prep and m == AT_K:
                        split(i + 2, 1, k_parts, rest[:, :])
                    if ffn and m + AHEAD < FFN_STEPS:
                        low_part(j, m + AHEAD)
                if i is not None:
                    if ffn:
                        pool.wait_ge(stored, i * STORE_INC)
                    pool.wait_ge(t2_done, i + 1)
                    pool.tensor_tensor(t2[:, :], t2_next, zero[:, :].broadcast_to([P, TOK]),
                                       ALU.add).then_inc(t2_copied, 1)

            for k in range(2):
                reciprocal_root(k, 0)
                split(k, 0, q_parts, x_in[:, 1 - k, :])
                split(k, 1, k_parts, rest[:, :])
            experts(0, None, False, True, True)
            with pool.Fori(1, IMAGES - 2) as i:
                experts(i, i - 1, True, True, True)
            experts(IMAGES - 2, IMAGES - 3, True, True, False)
            experts(IMAGES - 1, IMAGES - 2, True, False, False)
            experts(None, IMAGES - 1, True, False, False)

        @block.tensor
        def _(pe):
            def small(bank, rows, cols, lhs_t, rhs):
                return pe.matmul(ps[0:rows, bank, 0:cols], lhs_t, rhs, start=True, stop=True)

            pe.wait_ge(const_in, CONST_INC)
            pe.wait_ge(setup_dve, 1)
            small(0, P, IMAGES, group_mean, se[:, 0, :]).then_inc(setup_pe, 1)
            pe.wait_ge(setup_dve, 2)
            small(1, P, IMAGES, group_mean, se[:, 2, :]).then_inc(setup_pe, 1)
            pe.wait_ge(setup_dve, 4)
            small(2, SPLITS, IMAGES, split_mean[:, :], se[:, 5, :]).then_inc(setup_pe, 1)
            pe.wait_ge(setup_dve, 5)
            small(3, SPLITS, IMAGES, m1_t[:, :], se[0:SPLITS, 6, :]).then_inc(setup_pe, 1)
            small(4, SPLITS * HID, IMAGES, w1_blocks, se[:, 5, :]).then_inc(setup_pe, 1)
            pe.wait_ge(setup_dve, 6)
            small(5, SPLITS, IMAGES, m2_t[:, :], se[0:SPLITS, 7, :]).then_inc(setup_pe, 1)
            pe.wait_ge(setup_dve, 7)
            small(6, P, IMAGES, w2_blocks, se[0:SPLITS * HID, 8, :]).then_inc(setup_pe, 1)
            pe.wait_ge(setup_dve, 8)
            small(7, P, IMAGES, split_spread[:, :], se[0:SPLITS, 9, :]).then_inc(setup_pe, 1)
            small(0, P, P, wt_t, wo2).then_inc(setup_pe, 1)
            for e in range(EXPERTS):
                for f in range(FT):
                    n = e * FT + f
                    mm = pe.matmul(ps[:, 1, e:e + 1], w_out_raw[:, n * P:(n + 1) * P], b1[:, n:n + 1],
                                   start=(f == 0), stop=(f == FT - 1))
            mm.then_inc(setup_pe, 1)
            pe.wait_ge(setup_dve, 10)
            small(2, GATE_ROWS, P, bias9[:, :, :, :].rearrange("p c a b -> p (c a b)"), ident[:, :]).then_inc(setup_pe, 1)

            def turn_x(k):
                pe.wait_ge(x1_done, k + 1)
                for t in range(TILES):
                    mm = pe.transpose(tiles(SIDE_A)[:, t, :], x_in[:, 0, t * P:(t + 1) * P], ident[:, :])
                mm.then_inc(turned[0], 1)

            def turn_back_n1(k):
                pe.wait_ge(tok_done[0], k + 1)
                for t in range(TILES):
                    mm = pe.transpose(tiles(SIDE_A)[:, t, :], norm_tok[:, 0, t, :], ident[:, :])
                mm.then_inc(back[0], 1)

            def project(k, w, lo, ready):
                pe.wait_ge(norm_done, k + 1)
                for c in range(HALVES):
                    mm = pe.matmul(ps[:, lo + c, :], w[:, :], norm_ch[:, c * BANK:(c + 1) * BANK], start=True, stop=True)
                mm.then_inc(ready, 1)

            def values_and_z(k, r):
                if r:
                    pe.wait_ge(vz_done, k * 4 + 2)
                for t in range(4 * r, 4 * r + 4):
                    mm = pe.matmul(ps[:, SIDE_A + t // 2 % 2, (t % 2) * 2 * P:(t % 2 + 1) * 2 * P],
                                   norm_ch[:, t * P:(t + 1) * P], wvz[:, :], start=True, stop=True)
                    if t % 2:
                        mm.then_inc(vz_ready, 1)

            def full_scores(k, n, c, lo=None, pairs=1):
                h, t = divmod(n, TILES)
                if n % (2 * TILES) == 0 and c == 0:
                    pe.wait_ge(stack_in[h // 2], k * STACK_INC + STACK_INC)
                if n >= pairs:
                    pe.wait_ge(max_done, k * 2 * STEPS + 2 * (n - pairs) + c + 1)
                pe.matmul(ps[:, (max_bank(n) if lo is None else lo) + c, :], q_stack[0:SHIFT_ROW, h, t * P:(t + 1) * P],
                          k_stack[0:SHIFT_ROW, h, c * BANK:(c + 1) * BANK], start=True,
                          stop=True).then_inc(full_ready, 1)

            def turn_maxima(k, g):
                pe.wait_ge(max_joined, k * 2 + g + 1)
                pe.matmul(ps[0:GROUP_ROWS, SIDE_A, 0:P], row_max[:, g * GROUP_ROWS:(g + 1) * GROUP_ROWS], ident[:, :],
                          start=True, stop=True).then_inc(max_turned, 1)

            def turn_back_n2(j):
                pe.wait_ge(tok_done[1], j + 1)
                for t in range(TILES):
                    mm = pe.transpose(tiles(SIDE_A)[:, t, :], norm_tok[:, 1, t, :], ident[:, :])
                mm.then_inc(back[1], 1)

            def gate_logits(j):
                pe.wait_ge(n2_done, j + 1)
                for t in range(TILES):
                    for part in range(2):
                        mm = pe.matmul(ps[:, SIDE_A, t * EXPERTS:(t + 1) * EXPERTS],
                                       n2[:, part, t * P:(t + 1) * P].bitcast(F32), w_gate[:, :],
                                       start=(part == 0), stop=(part == 1))
                mm.then_inc(logits_ready, 1)

            def turn_gates(j):
                pe.wait_ge(gates_done, j + 1)
                for t in range(TILES):
                    mm = pe.transpose(ps[0:GATE_ROWS, SIDE_A + t // 4, (t % 4) * P:(t % 4 + 1) * P],
                                      gate9[:, t, :, :, :].rearrange("p c a b -> p (c a b)"), ident[:, :])
                mm.then_inc(gates_turned, 1)

            def scores(i, s):
                g, r = divmod(s, TILES * GROUP)
                t, h = r // GROUP, g * GROUP + r % GROUP
                if s == 0:
                    pe.wait_ge(shift_in, i * 2 * SHIFT_INC + SHIFT_INC)
                if s == STEPS // 2:
                    pe.wait_ge(shift_in, i * 2 * SHIFT_INC + 2 * SHIFT_INC)
                for c in range(HALVES):
                    mm = pe.matmul(ps[:, 2 * (s % 2) + c, :], k_stack[:, h, t * P:(t + 1) * P],
                                   q_stack[:, h, c * BANK:(c + 1) * BANK], start=True, stop=True)
                mm.then_inc(score_ready, 1)

            def values(i, u, c):
                g, t = divmod(u, TILES)
                if u == TILES:
                    pe.wait_ge(o_copied, i * 4 + c + 1)
                for r in range(GROUP):
                    mm = pe.matmul(ps[32 * r:32 * r + 32, O_BANKS + c, :], v_aug[:, t, g * GROUP + r, :],
                                   probs[:, u % 2, r, c * BANK:(c + 1) * BANK], start=(t == 0), stop=(t == TILES - 1))
                if t == TILES - 1:
                    mm.then_inc(half_done, 1)
                elif c == HALVES - 1:
                    mm.then_inc(value_done, 1)

            def values_at(i, s):
                u, r = divmod(s - GROUP + 1, GROUP)
                if u >= 0 and r in VALUES_AT:
                    values(i, u, VALUES_AT.index(r))

            def attention(i, j, ffn, nxt):
                pe.wait_ge(vz_done, i * 4 + 4)
                for s in range(STEPS):
                    if s + 2 < STEPS:
                        pe.wait_ge(exp_done, i * STEPS + s + 1)
                        scores(i, s + 2)
                    if s == AT_SHIFT2:
                        turn_maxima(i, 1)
                    if ffn and s == AT_BACK2:
                        pe.wait_ge(max_split, i * 2 + 2)
                        turn_back_n2(j)
                    if ffn and s == AT_LOGITS:
                        gate_logits(j)
                    if ffn and s == AT_GATES:
                        turn_gates(j)
                    if nxt and s == AT_FIRST:
                        pe.wait_ge(max_split, i * 2 + 2)
                        if ffn:
                            pe.wait_ge(gates_copied, j + 1)
                    for c in range(HALVES):
                        if s in MAX_SECOND:
                            full_scores(i, MAX_SECOND[s], c)
                        if nxt and s in MAX_FIRST:
                            full_scores(i + 1, MAX_FIRST[s], c)
                        if c == 0:
                            if s == STEPS - 1:
                                pe.wait_ge(exp_done, i * STEPS + STEPS)
                            values_at(i, s)
                for s in range(STEPS, STEPS + GROUP - 1):
                    values_at(i, s)

            def turn_o(i, g):
                if g == 0:
                    pe.wait_ge(o_copied, i * 4 + 4)
                else:
                    pe.wait_ge(o_scaled, i * 2 + 1)
                for t in range(TILES):
                    mm = pe.transpose(tiles(SIDE_B)[:, t, :], o_sb[g][:, t * P:(t + 1) * P], ident[:, :])
                mm.then_inc(o_turned, 1)

            def turn_back_o(i):
                pe.wait_ge(o_scaled, i * 2 + 2)
                for t in range(TILES):
                    mm = pe.transpose(tiles(SIDE_B)[:, t, :], on_tok[:, t, :], ident[:, :])
                mm.then_inc(on_back, 1)

            def decay_tile(i, t):
                if t == 0:
                    pe.wait_ge(on_done, i + 1)
                near = range(max(0, t - REACH), min(TILES, t + REACH + 1))
                for kt in near:
                    at = (t - kt + REACH) * P
                    pe.matmul(ps[:, SIDE_B + t // 4, (t % 4) * P:(t % 4 + 1) * P], z[:, kt, :], decay[:, at:at + P],
                              start=(t % 4 == 0 and kt == near[0]), stop=False)

            def project_out():
                for c in range(HALVES):
                    mm = pe.matmul(ps[:, SIDE_B + c, :], wo1[:, :], on_ch[:, c * BANK:(c + 1) * BANK],
                                   start=False, stop=True)
                mm.then_inc(attn_ready, 1)

            def turn_t2(i):
                pe.wait_ge(t2_done, i + 1)
                for t in range(TILES):
                    mm = pe.transpose(tiles(SIDE_B)[:, t, :], x_in[:, 1, t * P:(t + 1) * P], ident[:, :])
                mm.then_inc(turned[1], 1)

            def three_passes(bank, w, n, high, low, start, stop):
                pe.matmul(ps[:, bank, :], w[:, 0, n, :], high, start=start, stop=False)
                pe.matmul(ps[:, bank, :], w[:, 0, n, :], low, start=False, stop=False)
                return pe.matmul(ps[:, bank, :], w[:, 1, n, :], high, start=False, stop=stop)

            def first(j, m):
                c, n = divmod(m, SLICES)
                if m >= 2:
                    pe.wait_ge(hidden_done, j * FFN_STEPS + m - 1)
                at = slice(c * BANK, (c + 1) * BANK)
                three_passes(m % 2, w_in, n, n2[:, 0, at], n2[:, 1, at], True, True).then_inc(hidden_ready, 1)

            def second(j, m):
                c, n = divmod(m, SLICES)
                pe.wait_ge(low_done, j * FFN_STEPS + m + 1)
                three_passes(YB, w_out, n, hid_high[m % PART_BUFS], hid_low[m % PART_BUFS], False,
                             n == SLICES - 1).then_inc(hidden_used, 1)

            def wide(j, w):
                c, e = divmod(w, EXPERTS)
                if w >= 1:
                    pe.wait_ge(wide_done, j * WIDES + w)
                pe.matmul(ps[:, CB, :], pick_bf[:, e * P:(e + 1) * P], gate_t[0:3 * EXPERTS, c * BANK:(c + 1) * BANK],
                          start=True, stop=True).then_inc(wide_ready, 1)

            def biases(j, c):
                if c:
                    pe.wait_ge(result_done, j * HALVES + 1)
                pe.matmul(ps[:, YB, :], bias_rows[:, :], gate_t[:, c * BANK:(c + 1) * BANK], start=True, stop=False)

            def experts(i, j, ffn, nxt, prep):
                if ffn:
                    pe.wait_ge(gates_copied, j + 1)
                    wide(j, 0)
                    first(j, 0)
                    first(j, 1)
                    wide(j, 1)
                    first(j, 2)
                    biases(j, 0)
                for m in range(FFN_STEPS):
                    if nxt and m == AT_SHIFT1:
                        turn_maxima(i + 1, 0)
                    if nxt and m in MAX_BESIDE:
                        n = MAX_BESIDE[m]
                        if n == GROUP_ROWS:
                            pe.wait_ge(max_split, i * 2 + 3)
                        if n == MAX_ON_B[0]:
                            pe.wait_ge(tok_done[1], i + 1)
                        if n == MAX_AFTER_PREP:
                            pe.wait_ge(vz_done, i * 4 + 8)
                            if prep:
                                pe.wait_ge(norm_done, i + 3)
                        for c in range(HALVES):
                            full_scores(i + 1, n, c)
                    if i is not None:
                        if m in AT_TURN_O:
                            turn_o(i, AT_TURN_O.index(m))
                        if m == AT_BACK_O:
                            turn_back_o(i)
                        if m in DECAY_TILES:
                            for t in DECAY_TILES[m]:
                                decay_tile(i, t)
                        if m == AT_OUT:
                            project_out()
                        if m == AT_TURN_T2:
                            turn_t2(i)
                    if prep and m == AT_TURN_X:
                        pe.wait_ge(max_split, i * 2 + 3)
                        pe.wait_ge(max_done, (i + 1) * 2 * STEPS + 2 * MAX_ON_B[0])
                        turn_x(i + 2)
                    if nxt and m == AT_VZ[0]:
                        if prep:
                            pe.wait_ge(tok_done[0], i + 3)
                        else:
                            pe.wait_ge(max_split, i * 2 + 3)
                            pe.wait_ge(max_done, (i + 1) * 2 * STEPS + 2 * MAX_ON_B[0])
                        values_and_z(i + 1, 0)
                    if nxt and m == AT_VZ[1]:
                        values_and_z(i + 1, 1)
                    if prep:
                        if m == AT_BACK1:
                            pe.wait_ge(vz_done, i * 4 + 8)
                            turn_back_n1(i + 2)
                        if m == AT_Q:
                            pe.wait_ge(max_done, (i + 1) * 2 * STEPS + 2 * MAX_AFTER_PREP)
                            project(i + 2, wq, SIDE_B, q_ready)
                        if m == AT_K:
                            pe.wait_ge(dve_split, (i * 2 + 4) * SPLIT_CHAIN + 1)
                            project(i + 2, wk, SIDE_B, k_ready)
                    if ffn:
                        if m % 2 == 0 and m // 2 + 2 < WIDES:
                            wide(j, m // 2 + 2)
                        if m + AHEAD < FFN_STEPS:
                            first(j, m + AHEAD)
                        if m == SLICES:
                            biases(j, 1)
                        second(j, m)
                    if nxt and m == AT_NEXT:
                        if ffn:
                            pe.wait_ge(hidden_done, j * FFN_STEPS + FFN_STEPS)
                        scores(i + 1, 0)
                if prep:
                    pe.wait_ge(dve_split, (i * 2 + 5) * SPLIT_CHAIN + 1)
                if nxt and not prep:
                    pe.wait_ge(max_done, (i + 1) * 2 * STEPS + 2 * MAX_AFTER_PREP)
                if nxt:
                    for c in range(HALVES):
                        full_scores(i + 1, MAX_EARLY - 1, c)
                if ffn and i is not None:
                    pe.wait_ge(result_done, i * HALVES)
                if nxt:
                    scores(i + 1, 1)

            pe.wait_ge(setup_done, 1)
            pe.wait_ge(setup_pool, 3)
            turn_x(0)
            turn_back_n1(0)
            project(0, wq, SIDE_B, q_ready)
            values_and_z(0, 0)
            values_and_z(0, 1)
            pe.wait_ge(dve_split, 1)
            project(0, wk, SIDE_B, k_ready)
            pe.wait_ge(vz_done, 4)
            turn_x(1)
            turn_back_n1(1)
            pe.wait_ge(setup_done, 2)
            for n in range(MAX_EARLY):
                if n == QK_BESIDE[0]:
                    pe.wait_ge(dve_split, SPLIT_CHAIN + 1)
                    project(1, wq, SIDE_B, q_ready)
                if n == QK_BESIDE[1]:
                    pe.wait_ge(dve_split, 2 * SPLIT_CHAIN + 1)
                    project(1, wk, SIDE_B, k_ready)
                if n == GROUP_ROWS:
                    turn_maxima(0, 0)
                for c in range(HALVES):
                    full_scores(0, n, c, 2 * (n % 2), 2)
            pe.wait_ge(dve_split, 3 * SPLIT_CHAIN + 1)
            pe.wait_ge(max_done, 2 * MAX_EARLY)

            scores(0, 0)
            scores(0, 1)
            attention(0, None, False, True)
            experts(0, None, False, True, True)
            with pe.Fori(1, IMAGES - 2) as i:
                attention(i, i - 1, True, True)
                experts(i, i - 1, True, True, True)
            attention(IMAGES - 2, IMAGES - 3, True, True)
            experts(IMAGES - 2, IMAGES - 3, True, True, False)
            attention(IMAGES - 1, IMAGES - 2, True, False)
            experts(IMAGES - 1, IMAGES - 2, True, False, False)
            turn_back_n2(IMAGES - 1)
            gate_logits(IMAGES - 1)
            turn_gates(IMAGES - 1)
            experts(None, IMAGES - 1, True, False, False)

        @block.scalar
        def _(act):
            for n in range(X_BUFS):
                act.dma_start(x_buf[n], a["x"][n]).then_inc(x_setup_in[n], 16)
            with act.Fori(1, IMAGES // X_BUFS) as i:
                for n in range(X_BUFS):
                    act.wait_ge(stats_done, i * X_BUFS + n - X_BUFS + 1)
                    act.dma_start(x_buf[n], a["x"][i * X_BUFS + n]).then_inc(x_setup_in[n], 16)
            act.wait_ge(stats_done, IMAGES)
            act.dma_start(x_in[:, 0, :], a["x"][0]).then_inc(x_next_in, 16)
            act.wait_ge(setup_pe, 6)
            act.activation(se[0:SPLITS, 10, :], ps[0:SPLITS, 5, 0:IMAGES], ACT.Exp, scale=-1.0).then_inc(setup_act, 1)
            act.wait_ge(setup_pe, 7)
            act.activation(se[:, 11, :], ps[:, 6, 0:IMAGES], ACT.Exp, scale=-1.0).then_inc(setup_act, 1)
            act.wait_ge(setup_pool, 3)

            def affine(k):
                act.wait_ge(x_next_in, (k + 1) * 16)
                act.activation(x_in[:, 0, :], x_in[:, 0, :], ACT.Identity, scale=slope[:, bass.ds(k, 1)],
                               bias=offset[:, bass.ds(k, 1)]).then_inc(x1_done, 1)

            def residual(i):
                act.wait_ge(x_now_in, (i + 1) * 16)
                act.activation(x_in[:, 1, :], x_in[:, 1, :], ACT.Identity, scale=slope[:, bass.ds(i, 1)],
                               bias=offset[:, bass.ds(i, 1)]).then_inc(res_done, 1)

            def normalise(k, j, lo):
                act.wait_ge(rs_done[j], k + 1)
                for t in range(TILES):
                    last = act.activation(norm_tok[:, j, t, :], tiles(lo)[:, t, :], ACT.Identity,
                                          scale=norm_rs[:, j, 0, t:t + 1], bias=norm_rs[:, j, 2, t:t + 1])
                last.then_inc(tok_done[j], 1)

            def norm_out(k):
                act.wait_ge(back[0], k + 1)
                act.activation(norm_ch[:, :], flat(SIDE_A), ACT.Copy).then_inc(norm_done, 1)

            def high_part(k, lo, ready, parts, done):
                act.wait_ge(ready, k + 1)
                act.activation(parts[:, 0, :], flat(lo), ACT.Copy).then_inc(done, 1)

            def vz_out(k, r):
                for b in range(2 * r, 2 * r + 2):
                    act.wait_ge(vz_ready, k * 4 + b + 1)
                    pair = ps[:, SIDE_A + b % 2, :].rearrange("p (t w) -> p t w", t=2)
                    act.activation(v_aug[:, 2 * b:2 * b + 2, :, 0:DH],
                                   pair[:, :, 0:P].rearrange("p t (h d) -> p t h d", d=DH), ACT.Copy)
                    for t in range(2):
                        last = act.activation(z[:, 2 * b + t, :], pair[:, t, P:2 * P], ACT.Copy,
                                              scale=decay_norm[:, 2 * b + t:2 * b + t + 1])
                    last.then_inc(vz_done, 1)

            def n2_high_out(j):
                act.wait_ge(back[1], j + 1)
                act.activation(n2[:, 0, :], flat(SIDE_A), ACT.Copy).then_inc(n2_high, 1)

            def exp_gap(j):
                act.wait_ge(gap_done, j + 1)
                act.activation(gate_v[:, 3, :], gate_v[:, 2, :], ACT.Exp).then_inc(gap_exp, 1)

            def gates_out(j):
                act.wait_ge(gates_turned, j + 1)
                act.activation(gate_t[:, :], ps[0:GATE_ROWS, SIDE_A:SIDE_A + 2, :].rearrange("p a b -> p (a b)"),
                               ACT.Copy).then_inc(gates_copied, 1)

            def weights(i, s):
                u, r = divmod(s, GROUP)
                act.wait_ge(score_ready, i * STEPS + s + 1)
                if u >= 2 and r == 0:
                    if u - 2 < TILES - 1:
                        act.wait_ge(value_done, i * VALUES_INC + u - 1)
                    elif u - 2 == TILES - 1:
                        act.wait_ge(half_done, i * 4 + 2)
                    else:
                        act.wait_ge(value_done, i * VALUES_INC + u - 2)
                act.activation(probs[:, u % 2, r, :], flat(2 * (s % 2)), ACT.Exp,
                               scale=DH ** -0.5).then_inc(exp_done, 1)

            def attention(i, j, ffn, prep):
                if prep:
                    act.wait_ge(qk_split, i * 2 + 4)
                    act.dma_start(x_in[:, 0, :], a["x"][i + 2]).then_inc(x_next_in, 16)
                for s in range(STEPS):
                    if s == AT_LOAD:
                        if ffn:
                            act.wait_ge(t2_copied, i)
                        else:
                            act.wait_ge(qk_split, 1)
                        act.dma_start(x_in[:, 1, :], a["x"][i]).then_inc(x_now_in, 16)
                    if ffn and s == AT_BACK2 + 2:
                        n2_high_out(j)
                    if ffn and s == AT_LOGITS + GAP_LAG:
                        exp_gap(j)
                    if ffn and s == AT_GATES + 2:
                        gates_out(j)
                    if s > 0:
                        weights(i, s)

            def copy_o(i, c, nxt):
                act.wait_ge(half_done, i * 4 + 2 + c + 1)
                act.wait_ge(rows_out, i * ROWS_INC + (2 if nxt else 1) * ROWS_INC)
                act.activation(o_sb[1][:, c * BANK:(c + 1) * BANK], ps[:, O_BANKS + c, :],
                               ACT.Copy).then_inc(o_copied, 1)

            def high_hidden(j, m):
                act.wait_ge(hidden_done, j * FFN_STEPS + m + 1)
                if m >= PART_BUFS:
                    act.wait_ge(hidden_used, j * FFN_STEPS + m - PART_BUFS + 1)
                act.activation(hid_high[m % PART_BUFS], hidden[m % HID_BUFS], ACT.Copy).then_inc(high_done, 1)

            def wide_out(j, w):
                act.wait_ge(wide_ready, j * WIDES + w + 1)
                if w >= WIDE_BUFS:
                    act.wait_ge(hidden_done, j * FFN_STEPS + FT * (w - WIDE_BUFS + 1))
                act.activation(gate_wide[w % WIDE_BUFS], ps[:, CB, :], ACT.Copy).then_inc(wide_done, 1)

            def store(j, c):
                act.wait_ge(result_done, j * HALVES + c + 1)
                act.dma_start(out[j, :, c * BANK:(c + 1) * BANK], t2[:, c * BANK:(c + 1) * BANK]).then_inc(stored, 16)

            def experts(i, j, ffn, nxt, prep):
                if i is not None:
                    copy_o(i, 0, nxt)
                    copy_o(i, 1, nxt)
                if ffn:
                    wide_out(j, 0)
                    wide_out(j, 1)
                    for m in range(AHEAD):
                        high_hidden(j, m)
                for m in range(FFN_STEPS):
                    if i is not None and m == AT_RESIDUAL:
                        residual(i)
                    if prep and m == AT_AFFINE:
                        affine(i + 2)
                    if i is not None and m == AT_BACK_O:
                        act.wait_ge(on_back, i + 1)
                        act.activation(on_ch[:, :], flat(SIDE_B), ACT.Copy).then_inc(on_done, 1)
                    if i is not None and m == AT_NORM2:
                        normalise(i, 1, SIDE_B)
                    if prep and m == AT_NORM1:
                        normalise(i + 2, 0, SIDE_A)
                    if nxt and m in AT_VZ:
                        vz_out(i + 1, AT_VZ.index(m))
                    if prep:
                        if m == AT_BACK1:
                            norm_out(i + 2)
                        if m == AT_Q:
                            act.wait_ge(rows_out, i * ROWS_INC + 2 * ROWS_INC)
                            high_part(i + 2, SIDE_B, q_ready, q_parts, q_high)
                        if m == AT_K:
                            high_part(i + 2, SIDE_B, k_ready, k_parts, k_high)
                    if ffn:
                        if m % 2 == 0 and m // 2 + 2 < WIDES:
                            wide_out(j, m // 2 + 2)
                        if m + AHEAD < FFN_STEPS:
                            high_hidden(j, m + AHEAD)
                        if m == SLICES + 1:
                            store(j, 0)
                if nxt:
                    weights(i + 1, 0)
                if ffn:
                    store(j, 1)

            act.wait_ge(setup_done, 1)
            for k in range(2):
                affine(k)
                normalise(k, 0, SIDE_A)
                norm_out(k)
                if k == 0:
                    act.wait_ge(turned[0], 1)
                    act.dma_start(x_in[:, 0, :], a["x"][1]).then_inc(x_next_in, 16)
                else:
                    act.wait_ge(rows_out, ROWS_INC)
                high_part(k, SIDE_B, q_ready, q_parts, q_high)
                if k == 0:
                    vz_out(0, 0)
                    vz_out(0, 1)
                high_part(k, SIDE_B, k_ready, k_parts, k_high)
            weights(0, 0)
            attention(0, None, False, True)
            experts(0, None, False, True, True)
            with act.Fori(1, IMAGES - 2) as i:
                attention(i, i - 1, True, True)
                experts(i, i - 1, True, True, True)
            attention(IMAGES - 2, IMAGES - 3, True, False)
            experts(IMAGES - 2, IMAGES - 3, True, True, False)
            attention(IMAGES - 1, IMAGES - 2, True, False)
            experts(IMAGES - 1, IMAGES - 2, True, False, False)
            n2_high_out(IMAGES - 1)
            exp_gap(IMAGES - 1)
            gates_out(IMAGES - 1)
            experts(None, IMAGES - 1, True, False, False)
            act.wait_ge(stored, IMAGES * STORE_INC)

        @block.vector
        def _(dve):
            dve.wait_ge(dct_in, 16)
            dve.memset(k_stack[SHIFT_ROW:STACK, :, :], 1.0).then_inc(dot_done, 1)
            with dve.Fori(0, IMAGES // X_BUFS) as i:
                for n in range(X_BUFS):
                    done = i * X_BUFS + n
                    dve.wait_ge(x_setup_in[n], (i + 1) * 16)
                    for c in range(HALVES):
                        last = dve.bn_stats(stat13[:, n % 2, 6 * c:6 * c + 6], x_buf[n][:, c * BANK:(c + 1) * BANK])
                    last.then_inc(bn_done, 1)
                    dve.wait_ge(dot_done, done + 1)
                    dve.tensor_tensor_reduce(dot_out, x_buf[n], dct, 1.0, 0.0, ALU.mult, ALU.add,
                                             stat13[:, n % 2, 12:13]).then_inc(dot_done, 1)
                    dve.wait_ge(bn_done, done + 1)
                    dve.wait_ge(dot_done, done + 2)
                    dve.tensor_copy(stats[:, done, :], stat13[:, n % 2, :]).then_inc(stats_done, 1)
            dve.wait_ge(const_in, CONST_INC)
            dve.tensor_copy(pick_bf[:, :], picks)
            dve.wait_ge(stats_done, IMAGES)
            for n in range(IMAGES):
                last = dve.bn_aggr(moments[:, n, :], stats[:, n, 0:12])
            last.then_inc(aggr_done, 1)
            dve.wait_ge(aggr_done, 1)

            links = [0]

            def link(ins):
                links[0] += 1
                ins.then_inc(setup_chain, 1)
                dve.wait_ge(setup_chain, links[0])

            dve.tensor_copy(se[:, 0, :], moments[:, :, 0]).then_inc(setup_dve, 1)
            dve.wait_ge(setup_pe, 1)
            link(dve.tensor_copy(offset[:, :], ps[:, 0, 0:IMAGES]))
            link(dve.tensor_tensor(se[:, 1, :], se[:, 0, :], offset[:, :], ALU.subtract))
            link(dve.tensor_tensor(se[:, 1, :], se[:, 1, :], se[:, 1, :], ALU.mult))
            dve.tensor_tensor(se[:, 2, :], se[:, 1, :], moments[:, :, 1], ALU.add).then_inc(setup_dve, 1)
            dve.wait_ge(setup_pe, 2)
            dve.tensor_scalar(se[:, 3, :], ps[:, 1, 0:IMAGES], 1e-5, None, ALU.add).then_inc(setup_dve, 1)
            dve.wait_ge(setup_dve, 3)
            link(dve.tensor_scalar(se[:, 1, :], offset[:, :], dct_sum[:, 0:1], None, ALU.mult))
            link(dve.tensor_tensor(se[:, 1, :], stats[:, :, 12], se[:, 1, :], ALU.subtract))
            dve.wait_ge(setup_pool, 5)
            dve.tensor_tensor(se[:, 5, :], se[:, 1, :], se[:, 4, :], ALU.mult).then_inc(setup_dve, 1)
            dve.wait_ge(setup_pe, 3)
            dve.tensor_copy(se[0:SPLITS, 6, :], ps[0:SPLITS, 2, 0:IMAGES]).then_inc(setup_dve, 1)
            dve.wait_ge(setup_pe, 5)
            dve.tensor_scalar(se[0:SPLITS, 7, :], ps[0:SPLITS, 3, 0:IMAGES], 0.0, None, ALU.max).then_inc(setup_dve, 1)
            dve.tensor_scalar(se[0:SPLITS * HID, 8, :], ps[0:SPLITS * HID, 4, 0:IMAGES], 0.0, None,
                              ALU.max).then_inc(setup_dve, 1)
            dve.wait_ge(setup_act, 1)
            link(dve.tensor_scalar(se[0:SPLITS, 10, :], se[0:SPLITS, 10, :], 1.0, None, ALU.add))
            dve.reciprocal(se[0:SPLITS, 9, :], se[0:SPLITS, 10, :]).then_inc(setup_dve, 1)
            dve.wait_ge(setup_act, 2)
            link(dve.tensor_scalar(se[:, 11, :], se[:, 11, :], 1.0, None, ALU.add))
            link(dve.reciprocal(se[:, 11, :], se[:, 11, :]))
            dve.wait_ge(setup_pe, 8)
            link(dve.tensor_tensor(se[:, 1, :], se[:, 11, :], ps[:, 7, 0:IMAGES], ALU.mult))
            link(dve.tensor_tensor(se[:, 2, :], se[:, 1, :], se[:, 4, :], ALU.mult))
            link(dve.tensor_scalar(slope[:, :], se[:, 2, :], 1.0, None, ALU.add))
            link(dve.scalar_tensor_tensor(offset[:, :], se[:, 2, :], -1.0, offset[:, :], ALU.mult, ALU.mult))
            dve.wait_ge(setup_pe, 9)
            dve.tensor_copy(wvz[:, P:2 * P], ps[:, 0, 0:P]).then_inc(setup_dve, 1)
            dve.wait_ge(setup_pe, 10)
            link(dve.tensor_tensor(bias_rest[:, 0, :], b2_t[:, :], ps[:, 1, 0:EXPERTS], ALU.add))
            for r in range(3):
                link(dve.tensor_copy(bias_bf[:, :], bias_rest[:, r, :]))
                for copy in range(3):
                    link(dve.tensor_copy(bias9[:, r, copy, :], bias_bf[:, :]))
                if r < 2:
                    link(dve.tensor_tensor(bias_rest[:, r + 1, :], bias_rest[:, r, :], bias_bf[:, :], ALU.subtract))
            dve.sem_inc(setup_dve, 1)
            link(dve.tensor_scalar(neg_b1[:, :], b1[:, :], -1.0, None, ALU.mult))
            dve.wait_ge(setup_pe, 11)
            link(dve.tensor_copy(bias_rows[:, :], ps[0:GATE_ROWS, 2, 0:P]))
            dve.sem_inc(setup_done, 1)

            def moments_of(k, j, lo):
                v = norm_v[:, j]
                base = k * NORM_CHAIN
                dve.wait_ge(turned[j], k + 1)
                for t in range(TILES):
                    last = dve.bn_stats(norm6[:, j, t, :], tiles(lo)[:, t, :])
                last.then_inc(bn_taken[j], 1)
                dve.wait_ge(bn_taken[j], k + 1)
                even, odd, s_even, s_odd = (norm6[:, j, :, c] for c in (1, 4, 2, 5))
                dve.tensor_tensor(v[:, 0, :], even, odd, ALU.add)
                dve.tensor_tensor(v[:, 1, :], even, odd, ALU.subtract)
                dve.tensor_tensor(v[:, 2, :], s_even, s_odd, ALU.add).then_inc(norm_step[j], 1)
                dve.wait_ge(norm_step[j], base + 1)
                dve.tensor_scalar(v[:, 3, :], v[:, 0, :], 0.5, None, ALU.mult)
                dve.tensor_tensor(v[:, 4, :], v[:, 1, :], v[:, 1, :], ALU.mult).then_inc(norm_step[j], 1)
                dve.wait_ge(norm_step[j], base + 2)
                dve.scalar_tensor_tensor(v[:, 5, :], v[:, 4, :], P / 4.0, v[:, 2, :], ALU.mult,
                                         ALU.add).then_inc(norm_step[j], 1)
                dve.wait_ge(norm_step[j], base + 3)
                dve.tensor_scalar(v[:, 6, :], v[:, 5, :], 1.0 / P, 1e-5, ALU.mult, ALU.add).then_inc(norm_step[j], 1)

            def split(k, n, lo, high, parts, scratch):
                dve.wait_ge(high, k + 1)
                dve.tensor_tensor(scratch, flat(lo), parts[:, 0, :], ALU.subtract).then_inc(dve_split, 1)
                dve.wait_ge(dve_split, (k * 2 + n) * SPLIT_CHAIN + 1)
                dve.tensor_copy(parts[:, 1, :], scratch).then_inc(dve_split, 1)

            def maximum(k, n, lo=None):
                for c in range(HALVES):
                    dve.wait_ge(full_ready, k * 2 * STEPS + 2 * n + c + 1)
                    dve.tensor_reduce(half_max[:, c, n:n + 1], ps[:, (max_bank(n) if lo is None else lo) + c, :], AX.X,
                                      ALU.max).then_inc(max_done, 1)

            def shift(k, g):
                at = slice(g * GROUP_ROWS, (g + 1) * GROUP_ROWS)
                turn = k * 2 + g
                dve.wait_ge(max_done, k * 2 * STEPS + (g + 1) * STEPS)
                dve.tensor_tensor(row_max[:, at], half_max[:, 0, at], half_max[:, 1, at], ALU.max).then_inc(max_joined, 1)
                turned_max = ps[0:GROUP_ROWS, SIDE_A, 0:P]
                dve.wait_ge(max_turned, turn + 1)
                if not (isinstance(turn, int) and turn == 0):
                    dve.wait_ge(shift_in, turn * SHIFT_INC)
                dve.tensor_scalar(max_parts[:, 0, :], turned_max, -1.0, None, ALU.mult).then_inc(max_step, 1)
                dve.wait_ge(max_step, turn * MAX_CHAIN + 1)
                dve.scalar_tensor_tensor(max_rest[:, :], turned_max, -1.0, max_parts[:, 0, :], ALU.mult,
                                         ALU.subtract).then_inc(max_step, 1)
                dve.wait_ge(max_step, turn * MAX_CHAIN + 2)
                dve.tensor_copy(max_parts[:, 1, :], max_rest[:, :]).then_inc(max_step, 1)
                dve.wait_ge(max_step, turn * MAX_CHAIN + 3)
                dve.tensor_tensor(max_parts[:, 2, :], max_rest[:, :], max_parts[:, 1, :],
                                  ALU.subtract).then_inc(max_split, 1)

            def n2_low_out(j):
                dve.wait_ge(n2_high, j + 1)
                dve.tensor_tensor(n2[:, 1, :], flat(SIDE_A), n2[:, 0, :].bitcast(F32), ALU.subtract).then_inc(n2_done, 1)

            def choose(j):
                dve.wait_ge(logits_ready, j + 1)
                steps = [0]

                def then(ins, go=True):
                    steps[0] += 1
                    ins.then_inc(gate_step, 1)
                    if go:
                        dve.wait_ge(gate_step, j * GATE_CHAIN + steps[0])

                def by_expert(ap):
                    return ap.rearrange("p (t e) -> p t e", e=EXPERTS)

                def wide(ap):
                    return ap.unsqueeze(2).broadcast_to([P, TILES, EXPERTS])

                def copies(ap):
                    return ap.unsqueeze(2).broadcast_to([P, TILES, 3, EXPERTS])

                logits, is_best, score, rest_l = gate[:, 0, :], gate[:, 1, :], gate[:, 2, :], gate[:, 3, :]
                best, top, gap, weight = gate_v[:, 0, :], gate_v[:, 1, :], gate_v[:, 2, :], gate_v[:, 3, :]
                then(dve.tensor_tensor(logits, ps[:, SIDE_A, 0:TILES * EXPERTS], b_gate[:, :], ALU.add))
                then(dve.tensor_reduce(best, by_expert(logits), AX.X, ALU.max))
                for k in range(2):
                    src = logits if k == 0 else rest_l
                    value = best if k == 0 else gap
                    pick = gate[:, 4 + k, :]
                    then(dve.tensor_tensor(by_expert(is_best), by_expert(src), wide(value), ALU.is_equal))
                    then(dve.tensor_tensor(score, is_best, rank[:, :], ALU.mult))
                    then(dve.tensor_reduce(top, by_expert(score), AX.X, ALU.max))
                    then(dve.tensor_tensor(by_expert(pick), by_expert(rank[:, :]), wide(top), ALU.is_equal))
                    if k == 0:
                        then(dve.scalar_tensor_tensor(rest_l, pick, -3.0e38, logits, ALU.mult, ALU.add))
                        then(dve.tensor_reduce(gap, by_expert(rest_l), AX.X, ALU.max))
                dve.tensor_tensor(gate_v[:, 2, :], gap, best, ALU.subtract).then_inc(gap_done, 1)
                dve.wait_ge(gap_exp, j + 1)
                then(dve.tensor_scalar(gate_v[:, 4, :], weight, 1.0, None, ALU.add))
                then(dve.reciprocal(gate_v[:, 5, :], gate_v[:, 4, :]))
                then(dve.tensor_tensor(gate_v[:, 6, :], weight, gate_v[:, 5, :], ALU.mult))
                then(dve.tensor_tensor(by_expert(gate[:, 6, :]), by_expert(gate[:, 4, :]), wide(gate_v[:, 5, :]), ALU.mult),
                     go=False)
                then(dve.tensor_tensor(by_expert(gate[:, 7, :]), by_expert(gate[:, 5, :]), wide(gate_v[:, 6, :]), ALU.mult))
                then(dve.tensor_tensor(gate[:, 0, :], gate[:, 6, :], gate[:, 7, :], ALU.add))
                for r in range(2):
                    then(dve.tensor_copy(gate_bf[:, :], gate[:, r, :]))
                    then(dve.tensor_copy(gate9[:, :, :, r, :], copies(by_expert(gate_bf[:, :]))), go=False)
                    then(dve.tensor_tensor(gate[:, r + 1, :], gate[:, r, :], gate_bf[:, :], ALU.subtract))
                then(dve.tensor_copy(gate_bf[:, :], gate[:, 2, :]))
                dve.tensor_copy(gate9[:, :, :, 2, :], copies(by_expert(gate_bf[:, :]))).then_inc(gates_done, 1)
                assert steps[0] == GATE_CHAIN, steps[0]

            def copy_o(i, c, nxt):
                dve.wait_ge(half_done, i * 4 + c + 1)
                dve.wait_ge(qk_split, i * 2 + (4 if nxt else 2))
                dve.tensor_copy(o_sb[0][:, c * BANK:(c + 1) * BANK], ps[:, O_BANKS + c, :]).then_inc(o_copied, 1)

            def attention(i, j, ffn, nxt):
                for s in range(STEPS):
                    if s == AT_COPY_O[0]:
                        copy_o(i, 0, nxt)
                    if s == AT_COPY_O[1]:
                        copy_o(i, 1, nxt)
                    if s == AT_SHIFT2:
                        shift(i, 1)
                    if ffn and s == AT_BACK2:
                        n2_low_out(j)
                    if ffn and s == AT_LOGITS:
                        choose(j)
                    if s in MAX_SECOND:
                        maximum(i, MAX_SECOND[s])
                    if nxt and s in MAX_FIRST:
                        maximum(i + 1, MAX_FIRST[s])

            def scale_o(i, g):
                by_head = tiles(SIDE_B).rearrange("p t (r w) -> p t r w", w=32)
                dve.wait_ge(o_turned, i * 2 + g + 1)
                dve.reciprocal(o_recip[:, g, :, :], by_head[:, :, :, DH]).then_inc(recip_done, 1)
                dve.wait_ge(recip_done, i * 2 + g + 1)
                dve.tensor_tensor(on_tok.rearrange("p t (h d) -> p t h d", d=DH)[:, :, g * GROUP:(g + 1) * GROUP, :],
                                  by_head[:, :, :, 0:DH],
                                  o_recip[:, g, :, :].unsqueeze(3).broadcast_to([P, TILES, GROUP, DH]),
                                  ALU.mult).then_inc(o_scaled, 1)

            def add_attention(i):
                dve.wait_ge(attn_ready, i + 1)
                dve.wait_ge(res_done, i + 1)
                dve.scalar_tensor_tensor(t2_next, flat(SIDE_B), b_out[:, 0:1], x_in[:, 1, :], ALU.add,
                                         ALU.add).then_inc(t2_done, 1)

            def activate(j, m):
                n, w = m % SLICES, m // FT
                dve.wait_ge(hidden_ready, j * FFN_STEPS + m + 1)
                dve.wait_ge(wide_done, j * WIDES + w + 1)
                if m >= HID_BUFS:
                    dve.wait_ge(low_done, j * FFN_STEPS + m - HID_BUFS + 1)
                dve.scalar_tensor_tensor(hidden[m % HID_BUFS], ps[:, m % 2, :], neg_b1[:, n:n + 1],
                                         gate_wide[w % WIDE_BUFS], ALU.max, ALU.mult).then_inc(hidden_done, 1)

            def result(j, c):
                at = slice(c * BANK, (c + 1) * BANK)
                dve.wait_ge(hidden_used, j * FFN_STEPS + (c + 1) * SLICES)
                dve.wait_ge(t2_copied, j + 1)
                dve.tensor_tensor(t2[:, at], t2[:, at], ps[:, YB, :], ALU.add).then_inc(result_done, 1)

            def experts(i, j, ffn, nxt, prep):
                if ffn:
                    for m in range(AHEAD):
                        activate(j, m)
                for m in range(FFN_STEPS):
                    if ffn and m == SLICES:
                        result(j, 0)
                    if nxt and m == AT_SHIFT1:
                        shift(i + 1, 0)
                    if nxt and m in MAX_BESIDE:
                        maximum(i + 1, MAX_BESIDE[m])
                    if i is not None:
                        if m in AT_TURN_O:
                            scale_o(i, AT_TURN_O.index(m))
                        if m == AT_OUT:
                            add_attention(i)
                        if m == AT_TURN_T2 + 1:
                            moments_of(i, 1, SIDE_B)
                    if prep:
                        if m == AT_TURN_X + 1:
                            moments_of(i + 2, 0, SIDE_A)
                        if m == AT_Q:
                            split(i + 2, 0, SIDE_B, q_high, q_parts, q_rest)
                        if m == AT_K:
                            split(i + 2, 1, SIDE_B, k_high, k_parts, rest[:, :])
                    if ffn and m + AHEAD < FFN_STEPS:
                        activate(j, m + AHEAD)
                if ffn:
                    result(j, 1)
                if nxt:
                    maximum(i + 1, MAX_EARLY - 1)

            def weight_parts(w, raw):
                view = raw.rearrange("p (n c) -> p n c", c=P)
                link(dve.tensor_copy(w[:, 0, :, :], view))
                link(dve.tensor_tensor(w[:, 1, :, :], view, w[:, 0, :, :].bitcast(F32), ALU.subtract))

            moments_of(0, 0, SIDE_A)
            weight_parts(w_in, w_in_raw)
            split(0, 0, SIDE_B, q_high, q_parts, x_in[:, 1, :])
            split(0, 1, SIDE_B, k_high, k_parts, rest[:, :])
            moments_of(1, 0, SIDE_A)
            weight_parts(w_out, w_out_raw)
            dve.sem_inc(setup_done, 1)
            for n in range(MAX_EARLY):
                if n == QK_BESIDE[0]:
                    split(1, 0, SIDE_B, q_high, q_parts, q_rest)
                if n == QK_BESIDE[1]:
                    split(1, 1, SIDE_B, k_high, k_parts, rest[:, :])
                if n == GROUP_ROWS:
                    shift(0, 0)
                maximum(0, n, 2 * (n % 2))

            attention(0, None, False, True)
            experts(0, None, False, True, True)
            with dve.Fori(1, IMAGES - 2) as i:
                attention(i, i - 1, True, True)
                experts(i, i - 1, True, True, True)
            attention(IMAGES - 2, IMAGES - 3, True, True)
            experts(IMAGES - 2, IMAGES - 3, True, True, False)
            attention(IMAGES - 1, IMAGES - 2, True, False)
            experts(IMAGES - 1, IMAGES - 2, True, False, False)
            n2_low_out(IMAGES - 1)
            choose(IMAGES - 1)
            experts(None, IMAGES - 1, True, False, False)


_NAMES = ["L0_conv_W1", "L0_conv_W2", "L0_conv_M1", "L0_conv_M2", "L1_attn_W_qkv", "L1_attn_W_out",
          "L1_attn_b_out", "L1_ffn_w1", "L1_ffn_b1", "L1_ffn_w2", "L1_ffn_b2", "L1_ffn_wg", "L1_ffn_bg"]


def laid_out(x, w):
    c = np.ascontiguousarray
    qkvt, out = w["L1_attn_W_qkv"], w["L1_attn_W_out"].reshape(HEADS, 2, DH, P)
    w1_blocks = np.zeros((P, SPLITS * HID), np.float32)
    w2_blocks = np.zeros((SPLITS * HID, P), np.float32)
    for g in range(SPLITS):
        w1_blocks[g * CP_SPLIT:(g + 1) * CP_SPLIT, g * HID:(g + 1) * HID] = w["L0_conv_W1"][g].T
        w2_blocks[g * HID:(g + 1) * HID, g * CP_SPLIT:(g + 1) * CP_SPLIT] = w["L0_conv_W2"][g].T

    def by_dim(m):
        return c(m.reshape(P, HEADS, DH).transpose(0, 2, 1).reshape(P, P))

    return {
        "x": c(x.reshape(IMAGES, P, TOK)),
        "m1_t": c(w["L0_conv_M1"].T), "m2_t": c(w["L0_conv_M2"].T),
        "w1_blocks": w1_blocks, "w2_blocks": w2_blocks, "wo1": c(out[:, 0].reshape(P, P)),
        "wq": by_dim(qkvt[:, 0:P]), "wk": by_dim(qkvt[:, P:2 * P]), "wv": c(qkvt[:, 2 * P:3 * P]),
        "wt_t": c(qkvt[:, 3 * P:4 * P].T), "wo2": c(out[:, 1].reshape(P, P)),
        "b_out": c(w["L1_attn_b_out"].reshape(P, 1)),
        "w_in": c(w["L1_ffn_w1"].reshape(EXPERTS, P, FT, P).transpose(1, 0, 2, 3).reshape(P, SLICES * P)),
        "w_out": c(w["L1_ffn_w2"].reshape(EXPERTS, FT, P, P).transpose(2, 0, 1, 3).reshape(P, SLICES * P)),
        "b1": c(w["L1_ffn_b1"].reshape(SLICES, P).T), "b2_t": c(w["L1_ffn_b2"].T),
        "w_gate": c(w["L1_ffn_wg"]), "b_gate": c(np.broadcast_to(w["L1_ffn_bg"], (TILES, EXPERTS))),
    }


def kernel(**inputs):
    import concourse.bacc as bacc
    from concourse.bass_utils import run_bass_kernel_spmd

    x = np.asarray(inputs["x"])
    arrays = laid_out(x, {n: np.asarray(inputs[n]) for n in _NAMES})
    arrays.update(shape_constants())
    nc = bacc.Bacc("TRN2", target_bir_lowering=False, num_devices=1)
    a = {n: nc.dram_tensor(f"in_{n}", v.shape, F32, kind="ExternalInput").ap() for n, v in arrays.items()}
    out = nc.dram_tensor("out", (IMAGES, P, TOK), F32, kind="ExternalOutput").ap()
    build(nc, a, out)
    r = run_bass_kernel_spmd(nc, [{f"in_{n}": v for n, v in arrays.items()}], core_ids=[0])
    return r.results[0]["out"].reshape(x.shape)
```
